# Optimizing a Trainium2 kernel written in Bass

```python
import numpy as np
import jax
import jax.numpy as jnp

def _softmax(x, axis=-1):
    return jax.nn.softmax(x, axis=axis)

def _gelu(x):
    return jax.nn.gelu(x, approximate=True)

def _silu(x):
    return jax.nn.silu(x)

def _sigmoid(x):
    return jax.nn.sigmoid(x)

def _layernorm(x, axis=-1, eps=1e-05):
    m = jnp.mean(x, axis=axis, keepdims=True)
    v = jnp.var(x, axis=axis, keepdims=True)
    return (x - m) / jnp.sqrt(v + eps)

def _scatter_add(tgt, idx, src, axis=0):
    return tgt.at[idx].add(src)

def _segment_sum(src, seg, n):
    return jax.ops.segment_sum(src, seg, n)
kernel_name = 'mk_vit_tower_cls_d2_tok_img512_r4_07d670'

def setup_inputs(seed: int=0):
    np.random.seed(seed)
    _w = jnp.asarray

    def _rec_inputs():
        import jax
        import jax.numpy as jnp
        _rk = jax.random.key(seed)
        x = -0.000178447 + 0.99995 * jax.random.normal(jax.random.fold_in(_rk, 1), (64, 3, 176, 208), jnp.float32)
        cls_tok = 0.02 * jax.random.normal(jax.random.fold_in(_rk, 5), (1, 1, 128), jnp.float32)
        return (x, cls_tok)
    x, cls_tok = _rec_inputs()

    def _L0_tok_setup():
        import jax, jax.numpy as jnp
        import numpy as np
        P1, P2, C = (16, 16, 3)
        PW, PH = (176 // P1, 208 // P2)
        key = jax.random.key(seed)
        k1, k2, k3, k4, k5 = jax.random.split(key, 5)
        B, D = (64, 128)
        patch_dim = P1 * P2 * C
        return {'x': jax.random.normal(k1, (B, C, PW * P1, PH * P2), dtype=jnp.float32), 'W': jax.random.normal(k2, (D, patch_dim), dtype=jnp.float32) * 0.02, 'b': jax.random.normal(k3, (D,), dtype=jnp.float32) * 0.02, 'cls_token': jax.random.uniform(k4, (1, 1, D), dtype=jnp.float32), 'pos_emb': jax.random.normal(k5, (1, PW * PH + 1, 1), dtype=jnp.float32)}
    _L0_tok_all = _L0_tok_setup()
    _L0_tok_in = {k: v for k, v in _L0_tok_all.items() if k in ('W', 'b', 'cls_token', 'pos_emb')}
    del _L0_tok_all

    def _L0_attn_setup():
        import jax, jax.numpy as jnp
        import numpy as np
        import math
        D_MODEL = 128
        D_STATE = 16
        D_CONV = 4
        EXPAND = 2
        D_INNER = D_MODEL * EXPAND
        B, L = (2, 512)
        EPS = 1e-08

        def _silu(v):
            return v * jax.nn.sigmoid(v)

        def _causal_depthwise_conv(x_blc, conv_w, conv_b):
            lhs = jnp.transpose(x_blc, (0, 2, 1))
            out = jax.lax.conv_general_dilated(lhs, conv_w, window_strides=(1,), padding=[(D_CONV - 1, 0)], dimension_numbers=('NCH', 'OIH', 'NCH'), feature_group_count=D_INNER)
            out = out + conv_b[None, :, None]
            return jnp.transpose(out, (0, 2, 1))
        key = jax.random.key(seed)
        ks = jax.random.split(key, 10)
        s_in = 1.0 / math.sqrt(D_MODEL)
        s_x = 1.0 / math.sqrt(D_INNER)
        s_c = 1.0 / math.sqrt(D_CONV)
        return {'x': jax.random.normal(ks[0], (B, L, D_MODEL), jnp.float32), 'W_in': jax.random.uniform(ks[1], (D_MODEL, 2 * D_INNER), jnp.float32, -s_in, s_in), 'b_in': jax.random.uniform(ks[2], (2 * D_INNER,), jnp.float32, -s_in, s_in), 'conv_w': jax.random.uniform(ks[3], (D_INNER, 1, D_CONV), jnp.float32, -s_c, s_c), 'conv_b': jax.random.uniform(ks[4], (D_INNER,), jnp.float32, -s_c, s_c), 'W_x': jax.random.uniform(ks[5], (D_INNER, 2 * D_STATE + 1), jnp.float32, -s_x, s_x), 'b_x': jax.random.uniform(ks[6], (2 * D_STATE + 1,), jnp.float32, -s_x, s_x), 'A_log': jax.random.uniform(ks[7], (D_STATE,), jnp.float32, -math.log(D_STATE), -1.0), 'D': jnp.ones((D_INNER,), jnp.float32), 'W_out': jax.random.uniform(ks[8], (D_INNER, D_MODEL), jnp.float32, -s_x, s_x), 'b_out': jax.random.uniform(ks[9], (D_MODEL,), jnp.float32, -s_x, s_x)}
    _L0_attn_all = _L0_attn_setup()
    _L0_attn_in = {k: v for k, v in _L0_attn_all.items() if k in ('W_in', 'b_in', 'conv_w', 'conv_b', 'W_x', 'b_x', 'A_log', 'D', 'W_out', 'b_out')}
    del _L0_attn_all

    def _L0_ffn_setup():
        import jax, jax.numpy as jnp
        import numpy as np
        S, B, I, O, H, E, K = (128, 32, 128, 128, 128, 8, 2)

        def _expert(x_seq, Wi, Wh, b, Wo, bo):
            Bsz = x_seq.shape[1]
            Hd = Wh.shape[0]

            def step(carry, xt):
                h, c = carry
                gates = xt @ Wi + h @ Wh + b
                i_, f_, g_, o_ = jnp.split(gates, 4, axis=-1)
                c = jax.nn.sigmoid(f_) * c + jax.nn.sigmoid(i_) * jnp.tanh(g_)
                h = jax.nn.sigmoid(o_) * jnp.tanh(c)
                return ((h, c), h @ Wo + bo)
            init = (jnp.zeros((Bsz, Hd), x_seq.dtype), jnp.zeros((Bsz, Hd), x_seq.dtype))
            _, ys = jax.lax.scan(step, init, x_seq)
            return ys
        key = jax.random.key(seed)
        ks = jax.random.split(key, 6)
        s = 0.02
        return {'x': jax.random.normal(ks[0], (S, B, I), dtype=jnp.float32), 'router_w': jax.random.normal(ks[1], (I, E), dtype=jnp.float32) * s, 'router_b': jnp.zeros((E,), dtype=jnp.float32), 'Wi': jax.random.normal(ks[2], (E, I, 4 * H), dtype=jnp.float32) * s, 'Wh': jax.random.normal(ks[3], (E, H, 4 * H), dtype=jnp.float32) * s, 'b': jnp.zeros((E, 4 * H), dtype=jnp.float32), 'Wo': jax.random.normal(ks[4], (E, H, O), dtype=jnp.float32) * s, 'bo': jnp.zeros((E, O), dtype=jnp.float32)}
    _L0_ffn_all = _L0_ffn_setup()
    _L0_ffn_in = {k: v for k, v in _L0_ffn_all.items() if k in ('router_w', 'router_b', 'Wi', 'Wh', 'b', 'Wo', 'bo')}
    del _L0_ffn_all

    def _L1_attn_setup():
        import jax, jax.numpy as jnp
        import numpy as np
        NUM_HEADS = 8
        ATTENTION_SPAN = 128
        LOOKAHEAD = True
        NEG_INF = -1000000000.0

        def _band_mask(S: int) -> jnp.ndarray:
            idx = jnp.arange(S)
            m = jnp.abs(idx[None, :] - idx[:, None]) <= ATTENTION_SPAN
            if not LOOKAHEAD:
                m = m & (idx[None, :] <= idx[:, None])
            return m
        key = jax.random.key(seed)
        k1, k2, k3 = jax.random.split(key, 3)
        B, S, D = (4, 512, 128)
        x = jax.random.normal(k1, (B, S, D), dtype=jnp.float32)
        w_qkv = jax.random.normal(k2, (D, 3 * D), dtype=jnp.float32) * D ** (-0.5)
        w_proj = jax.random.normal(k3, (D, D), dtype=jnp.float32) * D ** (-0.5)
        return {'x': x, 'w_qkv': w_qkv, 'w_proj': w_proj}
    _L1_attn_all = _L1_attn_setup()
    _L1_attn_in = {k: v for k, v in _L1_attn_all.items() if k in ('w_qkv', 'w_proj')}
    del _L1_attn_all

    def _L1_ffn_setup():
        import jax, jax.numpy as jnp
        import numpy as np
        B, N, D, E = (8, 2048, 128, 8)
        H = 2 * D
        key = jax.random.key(seed)
        ks = jax.random.split(key, 7)
        s = 0.02
        return {'x': jax.random.normal(ks[0], (B, N, D), dtype=jnp.float32), 'W1': jax.random.normal(ks[1], (E, D, H), dtype=jnp.float32) * s, 'b1': jnp.zeros((E, H), dtype=jnp.float32), 'W2': jax.random.normal(ks[2], (E, H, D), dtype=jnp.float32) * s, 'b2': jnp.zeros((E, D), dtype=jnp.float32), 'Wg': jax.random.normal(ks[3], (D, E), dtype=jnp.float32) * s, 'bg': jnp.zeros((E,), dtype=jnp.float32)}
    _L1_ffn_all = _L1_ffn_setup()
    _L1_ffn_in = {k: v for k, v in _L1_ffn_all.items() if k in ('W1', 'b1', 'W2', 'b2', 'Wg', 'bg')}
    del _L1_ffn_all
    return {'x': x, 'cls_tok': cls_tok, 'L0_tok_W': _L0_tok_in['W'], 'L0_tok_b': _L0_tok_in['b'], 'L0_tok_cls_token': _L0_tok_in['cls_token'], 'L0_tok_pos_emb': _L0_tok_in['pos_emb'], 'L0_attn_W_in': _L0_attn_in['W_in'], 'L0_attn_b_in': _L0_attn_in['b_in'], 'L0_attn_conv_w': _L0_attn_in['conv_w'], 'L0_attn_conv_b': _L0_attn_in['conv_b'], 'L0_attn_W_x': _L0_attn_in['W_x'], 'L0_attn_b_x': _L0_attn_in['b_x'], 'L0_attn_A_log': _L0_attn_in['A_log'], 'L0_attn_D': _L0_attn_in['D'], 'L0_attn_W_out': _L0_attn_in['W_out'], 'L0_attn_b_out': _L0_attn_in['b_out'], 'L0_ffn_router_w': _L0_ffn_in['router_w'], 'L0_ffn_router_b': _L0_ffn_in['router_b'], 'L0_ffn_Wi': _L0_ffn_in['Wi'], 'L0_ffn_Wh': _L0_ffn_in['Wh'], 'L0_ffn_b': _L0_ffn_in['b'], 'L0_ffn_Wo': _L0_ffn_in['Wo'], 'L0_ffn_bo': _L0_ffn_in['bo'], 'L1_attn_w_qkv': _L1_attn_in['w_qkv'], 'L1_attn_w_proj': _L1_attn_in['w_proj'], 'L1_ffn_W1': _L1_ffn_in['W1'], 'L1_ffn_b1': _L1_ffn_in['b1'], 'L1_ffn_W2': _L1_ffn_in['W2'], 'L1_ffn_b2': _L1_ffn_in['b2'], 'L1_ffn_Wg': _L1_ffn_in['Wg'], 'L1_ffn_bg': _L1_ffn_in['bg']}

def reference(x, cls_tok, L0_tok_W, L0_tok_b, L0_tok_cls_token, L0_tok_pos_emb, L0_attn_W_in, L0_attn_b_in, L0_attn_conv_w, L0_attn_conv_b, L0_attn_W_x, L0_attn_b_x, L0_attn_A_log, L0_attn_D, L0_attn_W_out, L0_attn_b_out, L0_ffn_router_w, L0_ffn_router_b, L0_ffn_Wi, L0_ffn_Wh, L0_ffn_b, L0_ffn_Wo, L0_ffn_bo, L1_attn_w_qkv, L1_attn_w_proj, L1_ffn_W1, L1_ffn_b1, L1_ffn_W2, L1_ffn_b2, L1_ffn_Wg, L1_ffn_bg):
    import jax
    import jax.numpy as jnp

    def _L0_tok_ref(x, W, b, cls_token, pos_emb):
        import jax, jax.numpy as jnp
        import numpy as np
        P1, P2, C = (16, 16, 3)
        PW, PH = (176 // P1, 208 // P2)
        B = x.shape[0]
        patches = x.reshape(B, C, PW, P1, PH, P2)
        patches = patches.transpose(0, 2, 4, 3, 5, 1).reshape(B, PW * PH, P1 * P2 * C)
        proj = jnp.einsum('bnp,dp->bnd', patches, W) + b
        cls = jnp.broadcast_to(cls_token, (B, 1, cls_token.shape[-1]))
        out = jnp.concatenate([cls, proj], axis=1) + pos_emb
        return out

    def _L0_attn_ref(x, W_in, b_in, conv_w, conv_b, W_x, b_x, A_log, D, W_out, b_out):
        import jax, jax.numpy as jnp
        import numpy as np
        import math
        D_MODEL = 128
        D_STATE = 16
        D_CONV = 4
        EXPAND = 2
        D_INNER = D_MODEL * EXPAND
        B, L = (2, 512)
        EPS = 1e-08

        def _silu(v):
            return v * jax.nn.sigmoid(v)

        def _causal_depthwise_conv(x_blc, conv_w, conv_b):
            lhs = jnp.transpose(x_blc, (0, 2, 1))
            out = jax.lax.conv_general_dilated(lhs, conv_w, window_strides=(1,), padding=[(D_CONV - 1, 0)], dimension_numbers=('NCH', 'OIH', 'NCH'), feature_group_count=D_INNER)
            out = out + conv_b[None, :, None]
            return jnp.transpose(out, (0, 2, 1))
        xr = x @ W_in + b_in
        x_inner, res = jnp.split(xr, 2, axis=-1)
        xc = _silu(_causal_depthwise_conv(x_inner, conv_w, conv_b))
        BCdt = xc @ W_x + b_x
        B_sel = BCdt[..., :D_STATE]
        C_sel = BCdt[..., D_STATE:2 * D_STATE]
        dt = jax.nn.softplus(BCdt[..., -1:])
        A = -jnp.exp(A_log)
        A_bar = jnp.exp(dt * A[None, None, :])
        P = jnp.maximum(jnp.cumprod(A_bar, axis=1), EPS)
        u = B_sel[..., None] * xc[:, :, None, :]
        g = jnp.cumsum(u / P[..., None], axis=1)
        h = g * P[..., None]
        y = jnp.einsum('bls,blsd->bld', C_sel, h) + D[None, None, :] * xc
        y = y * _silu(res)
        return y @ W_out + b_out

    def _L0_ffn_ref(x, router_w, router_b, Wi, Wh, b, Wo, bo):
        import jax, jax.numpy as jnp
        import numpy as np
        S, B, I, O, H, E, K = (128, 32, 128, 128, 128, 8, 2)

        def _expert(x_seq, Wi, Wh, b, Wo, bo):
            Bsz = x_seq.shape[1]
            Hd = Wh.shape[0]

            def step(carry, xt):
                h, c = carry
                gates = xt @ Wi + h @ Wh + b
                i_, f_, g_, o_ = jnp.split(gates, 4, axis=-1)
                c = jax.nn.sigmoid(f_) * c + jax.nn.sigmoid(i_) * jnp.tanh(g_)
                h = jax.nn.sigmoid(o_) * jnp.tanh(c)
                return ((h, c), h @ Wo + bo)
            init = (jnp.zeros((Bsz, Hd), x_seq.dtype), jnp.zeros((Bsz, Hd), x_seq.dtype))
            _, ys = jax.lax.scan(step, init, x_seq)
            return ys
        S_, B_, I_ = x.shape
        N = S_ * B_
        flat_x = x.reshape(N, I_)
        logits = flat_x @ router_w + router_b
        top_vals, top_idx = jax.lax.top_k(logits, K)
        rw = jax.nn.softmax(top_vals, axis=1)
        mask = (top_idx.T[:, None, :] == jnp.arange(E)[None, :, None]).astype(x.dtype)
        expert_x = (mask[..., None] * flat_x[None, None]).reshape(K, E, S_, B_, I_)
        run_e = jax.vmap(_expert, in_axes=(0, 0, 0, 0, 0, 0))
        run_ke = jax.vmap(run_e, in_axes=(0, None, None, None, None, None))
        out = run_ke(expert_x, Wi, Wh, b, Wo, bo)
        out = out.reshape(K, E, N, -1)
        y = jnp.einsum('ken,nk,keno->no', mask, rw, out)
        return y.reshape(S_, B_, -1)

    def _L1_attn_ref(x, w_qkv, w_proj):
        import jax, jax.numpy as jnp
        import numpy as np
        NUM_HEADS = 8
        ATTENTION_SPAN = 128
        LOOKAHEAD = True
        NEG_INF = -1000000000.0

        def _band_mask(S: int) -> jnp.ndarray:
            idx = jnp.arange(S)
            m = jnp.abs(idx[None, :] - idx[:, None]) <= ATTENTION_SPAN
            if not LOOKAHEAD:
                m = m & (idx[None, :] <= idx[:, None])
            return m
        B, S, D = x.shape
        H = NUM_HEADS
        hd = D // H
        scale = D ** (-0.5)
        qkv = x @ w_qkv
        qkv = qkv.reshape(B, S, H, 3 * hd).transpose(0, 2, 1, 3)
        q, k, v = jnp.split(qkv, 3, axis=-1)
        scores = jnp.einsum('bhqd,bhkd->bhqk', q, k) * scale
        mask = _band_mask(S)[None, None, :, :]
        scores = scores + (1.0 - mask.astype(scores.dtype)) * NEG_INF
        attn = jax.nn.softmax(scores, axis=-1)
        out = jnp.einsum('bhqk,bhkd->bhqd', attn, v)
        out = out.transpose(0, 2, 1, 3).reshape(B, S, D)
        return out @ w_proj

    def _L1_ffn_ref(x, W1, b1, W2, b2, Wg, bg):
        import jax, jax.numpy as jnp
        import numpy as np
        B, N, D, E = (8, 2048, 128, 8)
        H = 2 * D
        Bs, Ns, Ds = x.shape
        xf = x.reshape(Bs * Ns, Ds)
        logits = xf @ Wg + bg
        idx = jnp.argmax(logits, axis=-1)
        out = jnp.zeros_like(xf)
        num_experts = W1.shape[0]
        for e in range(num_experts):
            h = jax.nn.relu(xf @ W1[e] + b1[e])
            y = h @ W2[e] + b2[e]
            out = jnp.where((idx == e)[:, None], y, out)
        return out.reshape(Bs, Ns, Ds)
    h = _L0_tok_ref(x, L0_tok_W, L0_tok_b, L0_tok_cls_token, L0_tok_pos_emb)
    h = jnp.concatenate([jnp.broadcast_to(cls_tok, (h.shape[0], 1, h.shape[2])), h], axis=1)
    h = h + _L0_attn_ref(_layernorm(h, axis=-1), L0_attn_W_in, L0_attn_b_in, L0_attn_conv_w, L0_attn_conv_b, L0_attn_W_x, L0_attn_b_x, L0_attn_A_log, L0_attn_D, L0_attn_W_out, L0_attn_b_out)
    h = h + _L0_ffn_ref(_layernorm(h, axis=-1), L0_ffn_router_w, L0_ffn_router_b, L0_ffn_Wi, L0_ffn_Wh, L0_ffn_b, L0_ffn_Wo, L0_ffn_bo)
    h = h + _L1_attn_ref(_layernorm(h, axis=-1), L1_attn_w_qkv, L1_attn_w_proj)
    h = h + _L1_ffn_ref(_layernorm(h, axis=-1), L1_ffn_W1, L1_ffn_b1, L1_ffn_W2, L1_ffn_b2, L1_ffn_Wg, L1_ffn_bg)
    return h

_drawn_inputs = setup_inputs


def setup_inputs(seed=0):
    import zlib

    import numpy as np

    out = dict(_drawn_inputs(seed))
    spreads = {'L0_attn_D': (1.0, 0.6),
     'L0_ffn_router_b': (0.0, 0.1),
     'L0_ffn_b': (0.0, 0.431),
     'L0_ffn_bo': (0.0, 0.1),
     'L1_ffn_b1': (0.0, 0.414),
     'L1_ffn_b2': (0.0, 0.1),
     'L1_ffn_bg': (0.0, 0.1)}
    factors = {'cls_tok': 4.096,
     'L0_attn_b_in': 4.393,
     'L0_attn_b_x': 3.431,
     'L0_attn_A_log': 2.716,
     'L0_ffn_Wi': 3.702,
     'L0_ffn_Wh': 8.0,
     'L0_ffn_Wo': 2.746}
    for name, (base, spread) in spreads.items():
        noise = np.random.default_rng([zlib.crc32(name.encode()), seed]).standard_normal(out[name].shape)
        drawn = base * np.exp(spread * noise) if base else spread * noise
        out[name] = jnp.asarray(drawn.astype(out[name].dtype))
    for name, factor in factors.items():
        out[name] = (out[name] * factor).astype(out[name].dtype)
    return out
```

```python
from contextlib import ExitStack

import numpy as np
import concourse.bass as bass
from concourse import mybir

F32, R32, BF16, U32 = mybir.dt.float32, mybir.dt.float32r, mybir.dt.bfloat16, mybir.dt.uint32
ALU, ACT, AX = mybir.AluOpType, mybir.ActivationFunctionType, mybir.AxisListType

D, T = 128, 145
PT = 2 * T
PAD = 384
TAIL = T - 128
E, NH, HD = 8, 8, 16
DS = 16
KC = 6
PAIR_UNITS = 16
LN_EPS = 1e-5
CUM_EPS_LOG = float(np.log(1e-8))
GATES = ("f", "i", "g", "o")
STEP_NAMES = {
    "pe_a": (
        "tok ln1 back1 in0 in1 in2 in3 wx tr0 mt0 y0 tr1 mt1 y1 out ln2 back2 logits owt bo "
    ).split(),
    "pe_b": (
        "f0 i0 g0 o0 f1 i1 g1 o1 z0 f2 i2 g2 o2 z1 f3 i3 g3 o3 z2 f4 i4 g4 o4 z3 f5 i5 g5 o5 z4 f6 i6 g6 o6 "
        "z5 f7 i7 g7 o7 z6 f8 i8 g8 o8 z7 f9 i9 g9 o9 z8 f10 i10 g10 o10 z9 f11 i11 g11 o11 z10 f12 i12 g12 "
        "o12 z11 f13 i13 g13 o13 z12 f14 i14 g14 o14 z13 f15 i15 g15 o15 z14 z15 "
    ).split(),
    "pe_c": (
        "ln3 back3 q0 q1 q2 q3 k0 k1 k2 k3 v0 s0_0 s1_0 s2_0 shift0 p0_0 p1_0 p2_0 pv0 v1 s0_1 s1_1 s2_1 "
        "shift1 p0_1 p1_1 p2_1 pv1 proj ln4 back4 logits oht up0 up1 down0 up2 down1 up3 down2 up4 down3 up5 "
        "down4 up6 down5 up7 down6 up8 down7 up9 down8 up10 down9 up11 down10 up12 down11 up13 down12 up14 "
        "down13 up15 down14 down15 emit "
    ).split(),
    "act_a": (
        "back1 in0 in1 in2 in3 th wx abs exp ln p tr0 tr1 back2 e_gap owt "
    ).split(),
    "act_b": (
        "f0 i0 g0 o0 f1 tc0 i1 g1 o1 f2 tc1 i2 g2 o2 f3 tc2 i3 g3 o3 f4 tc3 i4 g4 o4 f5 tc4 i5 g5 o5 f6 tc5 "
        "i6 g6 o6 f7 tc6 i7 g7 o7 f8 tc7 i8 g8 o8 f9 tc8 i9 g9 o9 f10 tc9 i10 g10 o10 f11 tc10 i11 g11 o11 "
        "f12 tc11 i12 g12 o12 f13 tc12 i13 g13 o13 f14 tc13 i14 g14 o14 f15 tc14 i15 g15 o15 tc15 "
    ).split(),
    "act_c": (
        "back3 q0 q1 q2 q3 k0 k1 k2 k3 v0 shift0 p0_0 p1_0 p2_0 v1 shift1 p0_1 p1_1 p2_1 back4 oht relu0 "
        "relu1 relu2 relu3 relu4 relu5 relu6 relu7 relu8 relu9 relu10 relu11 relu12 relu13 relu14 relu15 emit "
    ).split(),
    "dve_a": (
        "tok ln1_s ln1_mv ln1_x silu_res conv0 conv1 conv2 conv3 xc dt sum cum qk mt0 y0 yg0 mt1 y1 yg1 out "
        "ln2_s ln2_mv ln2_x lg top top_i gap e_sum w0 w1 ow1 ow owt bo "
    ).split(),
    "dve_b": (
        "take_hi take_lo ig0 c0 h0 hh0 hm0 hl0 ig1 c1 h1 hh1 hm1 hl1 ig2 c2 h2 hh2 hm2 hl2 ig3 c3 h3 hh3 hm3 "
        "hl3 ig4 c4 h4 hh4 hm4 hl4 ig5 c5 h5 hh5 hm5 hl5 ig6 c6 h6 hh6 hm6 hl6 ig7 c7 h7 hh7 hm7 hl7 ig8 c8 "
        "zz0 sum0 h2_0 h8 hh8 hm8 hl8 ig9 c9 h9 hh9 hm9 hl9 ig10 c10 h10 hh10 hm10 hl10 ig11 c11 h11 hh11 "
        "hm11 hl11 ig12 c12 h12 hh12 hm12 hl12 ig13 c13 h13 hh13 hm13 hl13 ig14 c14 h14 hh14 hm14 hl14 ig15 "
        "c15 h15 hh15 hm15 hl15 zz1 sum1 h2_1 "
    ).split(),
    "dve_c": (
        "take ln3_s ln3_mv ln3_x q0 q1 q2 q3 k0 k1 k2 k3 v0 s0_0 s1_0 s2_0 own_0 den0 inv0 on0 v1 s0_1 s1_1 "
        "s2_1 own_1 den1 inv1 on1 proj ln4_s ln4_mv ln4_x lg top top_i top_f oh oht moe "
    ).split(),
    "pool_a": (
        "ve1 rstd1 ve2 rstd2 "
    ).split(),
    "pool_b": (
        "mx0 mx1 mx2 mx3 mx4 mx5 mx6 mx7 mx8 mx9 mx10 mx11 mx12 mx13 mx14 mx15 "
    ).split(),
    "pool_c": (
        "ve3 rstd3 qt0 kt0 qt1 kt1 ve4 rstd4 hm0 hm1 hm2 hm3 hm4 hm5 hm6 hm7 hm8 hm9 hm10 hm11 hm12 hm13 hm14 "
        "hm15 "
    ).split(),
}



class Steps:

    def __init__(self, sem, names):
        self.sem, self.names, self.pos = sem, names, 0

    def done(self, instruction, name):
        assert self.names[self.pos] == name, (self.names[self.pos], name)
        self.pos = (self.pos + 1) % len(self.names)
        return instruction.then_inc(self.sem, 1)

    def at(self, q, name):
        return q * len(self.names) + (len(self.names) + self.names.index(name) + 1)


FIELDS = {
    "tok_w": KC * D, "in_w": 4 * D, "x_w": 2 * 80, "out_w": 2 * D, "lstm_out_w": E * D,
    "q_w": 4 * D, "k_w": 4 * D, "v_w": D, "proj_w": 2 * D, "router_w": E, "gate_w": E,
    "in_b": 4, "conv_w": 8, "conv_b": 2, "skip_d": 2,
    "out_b": 1, "lstm_b": 4 * E, "w1_b": 2 * E, "x_b": 1, "a_log": 1, "router_b": E, "gate_b": E,
    "bo": D, "b2": D,
    "ident": 128, "causal": T, "own_cols": 16, "own_row": 4, "tail_sel": 18, "iota": E, "q_lo": 1, "k_lo": 1,
    "minus_half": 3,
}
ONCE = {"tok_b": 1, "cls_a": 1, "cls_b": 1, "pos": T - 1, "band_main": 18, "band_tail": 18, "tail_heads": 2 * 128}


def field_at(fields, name):
    return sum(n for f, n in list(fields.items())[:list(fields).index(name)])


def schedule():
    a = [("tok",), ("ln", 1), ("ln_back", 1)] + [("in", k) for k in range(4)] + [("conv",), ("wx",), ("scan",)]
    for b in range(2):
        a += [("tr", b), ("mt", b), ("y", b)]
    a += [("out",), ("ln", 2), ("ln_back", 2), ("route",), ("owt",), ("bo",), ("scratch",)]
    c = [("take",), ("ln", 3), ("ln_back", 3)] + [("qk", w, p) for w in "qk" for p in range(4)]
    for b in range(2):
        c += [("v", b)] + [("smax", b, m) for m in range(3)] + [("shift", b)]
        c += [("prob", b, m) for m in range(3)] + [("pv", b)]
    c += [("proj",), ("ln", 4), ("ln_back", 4), ("gate",), ("oht",)]
    for n in range(2 * E):
        c += [("up", n)] + ([("down", n - 1)] if n else [])
    c += [("down", 2 * E - 1), ("emit",)]
    a, c = [("A", *s) for s in a], [("C", *s) for s in c]

    order = [("B", "take"), ("B", "mask_x", 0)]
    slots, na, nc_ = 4 * PAIR_UNITS, 0, 0
    for u in range(PAIR_UNITS):
        for g in range(4):
            order.append(("B", "gate", u, g))
            if g == 0 and u + 1 < PAIR_UNITS:
                order.append(("B", "mask_x", u + 1))
            if g == 0 and u:
                order.append(("B", "tanh_c", u - 1))
            if g == 1 and u:
                order.append(("B", "hidden", u - 1))
            if g == 2:
                order.append(("B", "cell", u))
            if g == 3 and u:
                order.append(("B", "expert_out", u - 1))
                if u == E:
                    order.append(("B", "step_out", 0))
                if u in (4, 8):
                    order.append(("B", "masks", u // 4 + 1))
            s = 4 * u + g + 1
            while na < len(a) and na < len(a) * s / (slots - 12):
                order.append(a[na])
                na += 1
            while nc_ < len(c) and nc_ < len(c) * s / slots:
                order.append(c[nc_])
                nc_ += 1
            if u == 13 and g == 0:
                assert na == len(a)
                order.append(("A", "masks", 0))
    last = PAIR_UNITS - 1
    order += [("B", "tanh_c", last), ("B", "hidden", last), ("B", "expert_out", last), ("B", "step_out", 1),
              ("A", "masks", 1)]
    return order


def build(nc, x_t, wh, wi, wmoe, packed, once, v_ones, out, scr_onehot, scr_weight, scr_moe):
    NP = x_t.shape[0] - 1
    ctx = ExitStack()
    with ctx:
        def sb(name, shape, dt=F32):
            return ctx.enter_context(nc.sbuf_tensor(name, shape, dt))

        def bank(name):
            return ctx.enter_context(nc.psum_tensor(name, [128, 512], F32))

        def sem(name):
            return ctx.enter_context(nc.semaphore(name))

        packed_sb = sb("packed_sb", [128, sum(FIELDS.values())])

        def field(name, rows=128):
            at = field_at(FIELDS, name)
            return packed_sb[0:rows, at:at + FIELDS[name]]

        wh_hi, wh_lo = sb("wh_hi", [128, E * 512], R32), sb("wh_lo", [128, E * 512], R32)
        wi_hi, wi_lo = sb("wi_hi", [128, E * 512], R32), sb("wi_lo", [128, E * 512], R32)
        moe_w = sb("moe_w", [128, 4, 512])
        ident = field("ident")
        ident_r = sb("ident_r", [128, 128], R32)
        band_main, band_tail = sb("band_main", [128, 18], R32), sb("band_tail", [128, 18], R32)
        tail_heads = sb("tail_heads", [8, 2, 128], R32)
        neg_a = sb("neg_a", [16, 1])
        scrap = sb("scrap", [128, 9])
        h_add = sb("h_add", [128, T])

        x_raw = sb("x_raw", [128, KC, PT])
        h_a = sb("h_a", [128, PAD])
        xn_a = sb("xn_a", [128, PAD])
        xt_a = sb("xt_a", [128, 3, 128])
        conv_in = sb("conv_in", [128, 2, 2, T + 3])
        xc = sb("xc", [128, 2, PT])
        th = sb("th", [128, 2, PT])
        gate = sb("gate", [128, 2, PT])
        ow_t = sb("ow_t", [26, PT])
        b16, c16 = ow_t[0:16, :], sb("c16", [16, PT])
        dt16, e16, s16 = xt_a[:, :, :].rearrange("p c d -> p (c d)")[0:16, 0:PT], th[0:16, 0, :], th[0:16, 1, :]

        def once_field(name, rows=128):
            at = field_at(ONCE, name)
            return gate[:, :, :].rearrange("p k t -> p (k t)")[0:rows, at:at + ONCE[name]]

        xc_t = sb("xc_t", [128, 512])
        mt = sb("mt", [128, T + TAIL])
        stats, mv = sb("stats", [128, 3, 6]), sb("mv", [128, 3, 2])
        ve, rstd = sb("ve", [128, 3]), sb("rstd", [128, 3])
        lg, top = sb("lg", [128, 3, 8]), sb("top", [128, 3, 8])
        top_i, top_f = sb("top_i", [128, 3, 8], U32), sb("top_f", [128, 3, 2])
        e_gap, e_sum = sb("e_gap", [128, 3]), sb("e_sum", [128, 3])
        ow = sb("ow", [128, 3, 26])
        ow_w = sb("ow_w", [128, 3, 8])
        ow_b = sb("ow_b", [24, PT], BF16)

        h1, h2 = sb("h1", [128, PT]), sb("h2", [128, PT])
        xb_hi, xb_lo = sb("xb_hi", [128, PT], R32), sb("xb_lo", [128, PT], R32)
        onehot = [sb(f"onehot{i}", [128, 4, 2, T], BF16) for i in range(2)]
        slot_w = [sb(f"slot_w{i}", [128, 2, T]) for i in range(2)]
        mx_hi, mx_lo = sb("mx_hi", [128, 2, PT], R32), sb("mx_lo", [128, 2, PT], R32)
        hh, hl = sb("hh", [128, E, PT], R32), sb("hl", [128, E, PT], R32)
        cell2 = sb("cell2", [128, E, PT])
        act4 = sb("act4", [128, 4, PT])
        hid2 = sb("hid2", [128, PT])
        hm = sb("hm", [128, PT])
        z_tmp = hm[:, :].rearrange("p (k t) -> p k t", k=2)

        h_c = sb("h_c", [128, PAD])
        xn_c = sb("xn_c", [128, PAD])
        xt_c = sb("xt_c", [128, 3, 128])
        stats_c, mv_c = sb("stats_c", [128, 3, 6]), sb("mv_c", [128, 3, 2])
        ve_c, rstd_c = sb("ve_c", [128, 3]), sb("rstd_c", [128, 3])
        qs, ks = sb("qs", [128, 4, PT + 2], R32), sb("ks", [128, 4, PT + 2], R32)
        qk_hi = sb("qk_hi", [128, PT], R32)
        q_tail, k_tail = sb("q_tail", [128, 4, 128], R32), sb("k_tail", [128, 4, 128], R32)
        v_main, v_tail = sb("v_main", [128, NH * 128]), sb("v_tail", [128, 2, 128])
        row_max, tail_max = sb("row_max", [128, 8]), sb("tail_max", [128, 2])
        tail_max_own = sb("tail_max_own", [128, 2, 4])
        shift_t = sb("shift_t", [8, T + 1], R32)
        prob = sb("prob", [128, NH * (T + 1)])
        prob_tail = sb("prob_tail", [128, 2, T])
        norm = sb("norm", [128, 2, PT])
        o_n = sb("o_n", [128, 2, PT])
        lg_c, top_c = sb("lg_c", [128, 3, 8]), sb("top_c", [128, 3, 8])
        top_ic, top_fc = sb("top_ic", [128, 3, 8], U32), sb("top_fc", [128, 3, 1])
        oh_c, oh_b = sb("oh_c", [128, 3, 8]), sb("oh_b", [8, PT], BF16)
        oh_t = xt_c[:, :, :].rearrange("p c d -> p (c d)")[0:8, 0:PT]
        out_sb = sb("out_sb", [128, 3, 128])
        relu2, hm2 = norm, o_n
        onehot_c = prob[:, :].bitcast(BF16)[:, 0:E * PT].rearrange("p (e t) -> p e t", e=E)

        gates = [bank(f"gate_{g}") for g in GATES]
        z_bank, m_bank, a_bank, c_bank = bank("z_bank"), bank("m_bank"), bank("a_bank"), bank("c_bank")

        steps = {}
        for eng, chains in (("pe", "abc"), ("act", "abc"), ("dve", "abc"), ("pool", "abc")):
            for ch in chains:
                key = f"{eng}_{ch}"
                steps[key] = Steps(sem(f"{key}_done"), STEP_NAMES[key])
        pe_a, pe_b, pe_c = steps["pe_a"], steps["pe_b"], steps["pe_c"]
        act_a, act_b, act_c = steps["act_a"], steps["act_b"], steps["act_c"]
        dve_a, dve_b, dve_c = steps["dve_a"], steps["dve_b"], steps["dve_c"]
        pool_a, pool_b, pool_c = steps["pool_a"], steps["pool_b"], steps["pool_c"]
        consts_in, once_in, ones_in, x_in = sem("consts_in"), sem("once_in"), sem("ones_in"), sem("x_in")
        stage_in = [sem(f"stage_in{i}") for i in range(2)]
        split_done, setup_split, setup_misc = sem("split_done"), sem("setup_split"), sem("setup_misc")
        waited = sem("waited")
        moe_in = [sem(f"moe_in{i}") for i in range(4)]
        scratch_out, onehot_in = sem("scratch_out"), [sem(f"onehot_in{i}") for i in range(2)]
        slot_w_in = [sem(f"slot_w_in{i}") for i in range(2)]
        scratch_c_out, onehot_c_in, out_stored = sem("scratch_c_out"), sem("onehot_c_in"), sem("out_stored")

        order = schedule()

        def run(eng, stages):
            def iteration(it, chains):
                for chain, name, *args in order:
                    part = stages.get((chain, name))
                    if chain in chains and part:
                        part(it + {"A": 1, "B": 0, "C": -1}[chain], *args)

            iteration(-1, "A")
            iteration(0, "AB")
            with eng.Fori(1, NP - 1) as it:
                iteration(it, "ABC")
            iteration(NP - 1, "BC")
            iteration(NP, "C")

        def first(q):
            return isinstance(q, int) and q == 0

        def after(eng, who, q, name):
            eng.wait_ge(who.sem, who.at(q, name))

        def before(eng, who, q, name):
            eng.wait_ge(who.sem, who.at(q, name) - len(who.names))

        def plain(eng):
            eng.sem_inc(waited, 1)

        def two(ap):
            return ap.rearrange("p (b t) -> p b t", b=2)

        def rows(head):
            side = head % 2
            return slice(64 * side, 64 * side + 64)

        def spread(ap, axis, n):
            ap = ap.unsqueeze(axis)
            shape = list(ap.shape)
            shape[axis] = n
            return ap.broadcast_to(shape)

        def heads_of(m, side):
            return range(side, 6, 2) if m == 0 else range(6 + side, 7 + side)

        def per_head(bank_, n):
            return bank_[:, 0:n * (T + 1)].rearrange("p (h t) -> p h t", t=T + 1)[:, :, 0:T]

        def dram_rows(ap, rows_, dims, offset=0):
            return bass.AP(ap.tensor, offset, [[0, rows_]] + dims)

        block = ctx.enter_context(nc.Block())

        @block.sync
        def _(sp):
            sp.dma_start(packed_sb[:, :], packed).then_inc(consts_in, 16)
            sp.dma_start(gate[:, :, :].rearrange("p k t -> p (k t)")[:, 0:sum(ONCE.values())], once
                         ).then_inc(once_in, 16)
            stage = cell2[:, :, :].rearrange("p e t -> p (e t)")
            for c in range(8):
                src = (wh if c < 4 else wi)[:, (c % 4) * 1024:(c % 4 + 1) * 1024]
                if c >= 2:
                    sp.wait_ge(split_done, c - 1)
                sp.dma_start(stage[:, (c % 2) * 1024:(c % 2 + 1) * 1024], src).then_inc(stage_in[c % 2], 16)
                if c == 1:
                    sp.dma_start(x_raw[:, :, :], x_t[0]).then_inc(x_in, 16)
                    sp.dma_start(v_main[:, :], v_ones[:, 0:1024]).then_inc(ones_in, 16)
                    sp.dma_start(v_tail[:, :, :].rearrange("p g c -> p (g c)"), v_ones[:, 1024:1280]).then_inc(ones_in, 16)
            for e in range(4):
                sp.dma_start(moe_w[:, e, :], wmoe[e]).then_inc(moe_in[e], 16)

            def load_x(q):
                after(sp, pe_a, q, "tok")
                sp.dma_start(x_raw[:, :, :], x_t[q + 1]).then_inc(x_in, 16)

            def scratch(q):
                after(sp, act_a, q, "owt")
                after(sp, dve_a, q, "owt")
                plain(sp)
                if not first(q):
                    for i in range(2):
                        sp.wait_ge(onehot_in[i], 32 * q)
                        sp.wait_ge(slot_w_in[i], 16 * q)
                for k in range(2):
                    sp.dma_start(scr_onehot[:, :, k, :].rearrange("b e t -> e b t"),
                                 two(ow_b[8 + 8 * k:16 + 8 * k, :])).then_inc(scratch_out, 16)
                sp.dma_start(scr_weight.rearrange("b k t -> k b t"), two(ow_t[24:26, :])).then_inc(scratch_out, 16)

            def load_onehot(q, hs):
                b, half = hs // 2, hs % 2
                sp.dma_start(onehot[half][:, :, :, :].rearrange("p e k t -> p (e k t)"),
                             dram_rows(scr_onehot, 128, [[1, 8 * T]], (b * E + 4 * half) * 2 * T)
                             ).then_inc(onehot_in[half], 16)

            def masks_a(q, b):
                if b == 0:
                    sp.wait_ge(scratch_out, q * 48 + 48)
                    plain(sp)
                if not first(q):
                    after(sp, dve_b, q - 1, f"hm{11 + 4 * b}")
                load_onehot(q, b)
                if not first(q):
                    after(sp, dve_b, q - 1, f"zz{b}")
                sp.dma_start(slot_w[b][:, :, :].rearrange("p k t -> p (k t)"),
                             dram_rows(scr_weight, 128, [[1, PT]], b * PT)).then_inc(slot_w_in[b], 16)

            def masks_b(q, hs):
                after(sp, dve_b, q, f"hm{4 * hs - 5}")
                load_onehot(q, hs)

            def scratch_c(q):
                after(sp, act_c, q, "oht")
                after(sp, dve_c, q, "oht")
                sp.dma_start(scr_moe, oh_b[:, :]).then_inc(scratch_c_out, 16)
                sp.wait_ge(scratch_c_out, q * 16 + 16)
                sp.dma_start(onehot_c, dram_rows(scr_moe, 128, [[PT, E], [1, PT]])).then_inc(onehot_c_in, 16)

            def moe_next(q, n):
                if n % 2:
                    e = n // 2
                    after(sp, pe_c, q, f"down{n}")
                    sp.dma_start(moe_w[:, e % 4, :], wmoe[(e + 4) % E]).then_inc(moe_in[e % 4], 16)

            def emit(q):
                after(sp, act_c, q, "emit")
                base = q * PT
                sp.dma_start(out[bass.ds(base, 256), :].rearrange("(c p) d -> p c d", c=2), out_sb[:, 0:2, :]
                             ).then_inc(out_stored, 16)
                sp.dma_start(out[bass.ds(base + 256, PT - 256), :], out_sb[0:PT - 256, 2, :]).then_inc(out_stored, 16)
                sp.wait_ge(out_stored, q * 32 + 32)
                plain(sp)

            run(sp, {("A", "tok"): load_x, ("A", "scratch"): scratch, ("A", "masks"): masks_a,
                     ("B", "masks"): masks_b, ("C", "oht"): scratch_c, ("C", "down"): moe_next, ("C", "emit"): emit})
            sp.wait_ge(out_stored, 32 * NP)
            sp.wait_ge(scratch_out, 48 * NP)
            sp.wait_ge(scratch_c_out, 16 * NP)
            sp.wait_ge(x_in, 16 * (NP + 1))
            for i in range(4):
                sp.wait_ge(moe_in[i], 16 * (2 * NP + 1))

        @block.tensor
        def _(pe):
            pe.wait_ge(consts_in, 16)
            pe.wait_ge(setup_misc, 1)
            for who, where in ((pe_a, a_bank), (pe_c, c_bank), (pe_b, z_bank)):
                pe.matmul(where[:, 0:128], ident, ident, start=True, stop=True).then_inc(who.sem, len(who.names))

            def transposes(src, dst, where):
                for c in range(3):
                    last = pe.transpose(where[:, c * 128:(c + 1) * 128], src[c], ident)
                return last

            def chunks(tile):
                return [tile[:, c * 128:(c + 1) * 128] for c in range(3)]

            def tok(q):
                pe.wait_ge(x_in, q * 16 + 16)
                before(pe, dve_a, q, "bo")
                for c in range(KC):
                    last = pe.matmul(a_bank[:, 0:PT], field("tok_w")[:, c * D:(c + 1) * D], x_raw[:, c, :],
                                     start=c == 0, stop=c == KC - 1)
                pe_a.done(last, "tok")

            def ln(who, dve, src, where, ready):
                def part(q, n):
                    after(pe, dve, q, ready[n])
                    who.done(transposes(chunks(src), None, where), f"ln{n}")
                return part

            def ln_back(who, dve, xt, where):
                def part(q, n):
                    after(pe, dve, q, f"ln{n}_x")
                    who.done(transposes([xt[:, c, :] for c in range(3)], None, where), f"back{n}")
                return part

            def in_proj(q, k):
                after(pe, act_a, q, f"in{k - 1}" if k else "back1")
                pe_a.done(pe.matmul(a_bank[:, 0:PT], field("in_w")[:, k * D:(k + 1) * D], xn_a[:, 0:PT],
                                    start=True, stop=True), f"in{k}")

            def wx(q):
                after(pe, act_a, q, "in3")
                after(pe, dve_a, q, "xc")
                for k in range(2):
                    last = pe.matmul(a_bank[0:80, 0:PT], field("x_w")[:, k * 80:(k + 1) * 80], xc[:, k, :],
                                     start=k == 0, stop=k == 1)
                pe_a.done(last, "wx")

            def tr(q, b):
                if b == 0:
                    after(pe, act_a, q, "wx")
                else:
                    after(pe, dve_a, q, "yg0")
                for k in range(2):
                    pe.transpose(a_bank[:, k * 128:(k + 1) * 128], xc[:, k, b * T:b * T + 128], ident)
                    last = pe.transpose(a_bank[0:TAIL, 256 + k * 128:384 + k * 128],
                                        xc[:, k, b * T + 128:b * T + T], ident)
                pe_a.done(last, f"tr{b}")

            def mt_part(q, b):
                after(pe, act_a, q, f"tr{b}")
                after(pe, dve_a, q, "qk")
                pe.matmul(a_bank[:, 0:T], b16[:, b * T:b * T + 128], c16[:, b * T:b * T + T], start=True, stop=True)
                pe_a.done(pe.matmul(a_bank[0:TAIL, T:T + TAIL], b16[:, b * T + 128:b * T + T],
                                    c16[:, b * T + 128:b * T + T], start=True, stop=True), f"mt{b}")

            def y(q, b):
                after(pe, dve_a, q, f"mt{b}")
                for k in range(2):
                    pe.matmul(a_bank[:, k * T:k * T + T], xc_t[:, k * 128:(k + 1) * 128], mt[:, 0:T],
                              start=True, stop=False)
                    last = pe.matmul(a_bank[:, k * T + 128:k * T + T], xc_t[0:TAIL, 256 + k * 128:384 + k * 128],
                                     mt[0:TAIL, T:T + TAIL], start=False, stop=True)
                pe_a.done(last, f"y{b}")

            def out_proj(q):
                after(pe, dve_a, q, "yg1")
                for k in range(2):
                    last = pe.matmul(a_bank[:, 0:PT], field("out_w")[:, k * D:(k + 1) * D], gate[:, k, :],
                                     start=k == 0, stop=k == 1)
                pe_a.done(last, "out")

            def logits(who, act, xn, w, where, name, evac):
                def part(q):
                    after(pe, act, q, evac)
                    for c in range(3):
                        last = pe.matmul(where[:, c * 8:c * 8 + 8], xn[:, c * 128:(c + 1) * 128], field(w),
                                         start=True, stop=True)
                    who.done(last, name)
                return part

            def owt(q):
                after(pe, dve_a, q, "ow")
                for c in range(3):
                    last = pe.matmul(a_bank[0:26, c * 128:(c + 1) * 128], ow[:, c, :], ident, start=True, stop=True)
                pe_a.done(last, "owt")

            def bo(q):
                after(pe, act_a, q, "owt")
                after(pe, dve_a, q, "owt")
                pe_a.done(pe.matmul(a_bank[:, 0:PT], field("bo", 8), ow_t[0:8, :], start=True, stop=True), "bo")

            def gate_part(q, u, g):
                e = u % E
                if u:
                    after(pe, act_b, q, f"{GATES[g]}{u - 1}")
                else:
                    before(pe, act_b, q, f"{GATES[g]}{PAIR_UNITS - 1}")
                if g == 0:
                    after(pe, pool_b, q, f"mx{u}")
                    if u < E:
                        before(pe, dve_b, q, f"hl{u + E}")
                    else:
                        after(pe, dve_b, q, f"hl{u - E}")
                w = slice(e * 512 + g * 128, e * 512 + (g + 1) * 128)
                parts = ((wi_hi, mx_hi[:, u % 2, :]), (wi_lo, mx_hi[:, u % 2, :]), (wi_hi, mx_lo[:, u % 2, :]),
                         (wh_hi, hh[:, e, :]), (wh_lo, hh[:, e, :]), (wh_hi, hl[:, e, :]))
                for n, (weight, moving) in enumerate(parts):
                    last = pe.matmul(gates[g][:, 0:PT], weight[:, w], moving, start=n == 0, stop=n == 5)
                pe_b.done(last, f"{GATES[g]}{u}")

            def expert_out(q, u):
                e = u % E
                after(pe, dve_b, q, f"hm{u}")
                if e == 0:
                    if u:
                        after(pe, dve_b, q, "zz0")
                    else:
                        before(pe, dve_b, q, "zz1")
                pe_b.done(pe.matmul(z_bank[:, 0:PT], field("lstm_out_w")[:, e * D:(e + 1) * D], hm[:, :],
                                    start=e == 0, stop=e == E - 1), f"z{u}")

            def qk(q, w, p):
                if (w, p) == ("q", 0):
                    after(pe, act_c, q, "back3")
                else:
                    after(pe, dve_c, q, f"{w}{p - 1}" if p else "q3")
                pe_c.done(pe.matmul(c_bank[:, 0:PT], field(f"{w}_w")[:, p * 128:(p + 1) * 128], xn_c[:, 0:PT],
                                    start=True, stop=True), f"{w}{p}")

            def v(q, b):
                after(pe, dve_c, q, "on0" if b else "k3")
                pe.matmul(c_bank[:, 0:128], xn_c[:, b * T:b * T + 128], field("v_w"), start=True, stop=True)
                for j in range(4):
                    last = pe.matmul(c_bank[32 * j:32 * j + 32, 128:256], xn_c[:, b * T + 128:b * T + 160],
                                     field("v_w"), start=True, stop=True)
                pe_c.done(last, f"v{b}")

            def smax(q, b, m):
                if m == 0:
                    after(pe, act_c, q, f"v{b}")
                    after(pe, dve_c, q, f"v{b}")
                    before(pe, dve_c, q, "moe")
                else:
                    after(pe, dve_c, q, f"s{m - 1}_{b}")
                cols = slice(b * T, b * T + T + 1)
                if m < 2:
                    for n in range(len(heads_of(m, 0))):
                        at = n * (T + 1)
                        for side, where in enumerate((c_bank, m_bank)):
                            h = heads_of(m, side)[n]
                            pe.matmul(where[:, at:at + T + 1], qs[rows(h), h // 2, b * T:b * T + 128],
                                      ks[rows(h), h // 2, cols], start=True, stop=False)
                        for where in (c_bank, m_bank):
                            last = pe.matmul(where[:, at + 128:at + 146], ident_r[:, :], band_main[:, :],
                                             start=False, stop=True)
                else:
                    after(pe, pool_c, q, f"kt{b}")
                    for g in range(2):
                        at = g * (T + 1)
                        for r in range(2):
                            pe.matmul(c_bank[:, at:at + T + 1], q_tail[:, 2 * g + r, :], ks[:, 2 * g + r, cols],
                                      start=r == 0, stop=False)
                        last = pe.matmul(c_bank[:, at:at + 18], ident_r[:, :], band_tail[:, :], start=False, stop=True)
                pe_c.done(last, f"s{m}_{b}")

            def shift(q, b):
                after(pe, dve_c, q, f"own_{b}")
                pe.matmul(c_bank[0:8, 0:128], row_max[:, :], ident, start=True, stop=True)
                pe_c.done(pe.matmul(c_bank[0:8, 128:146], tail_max_own[:, :, :].rearrange("p g j -> p (g j)"),
                                    field("tail_sel"), start=True, stop=True), f"shift{b}")

            def prob_part(q, b, m):
                after(pe, act_c, q, f"p{m - 1}_{b}" if m else f"shift{b}")
                cols = slice(b * T, b * T + T + 1)
                if m < 2:
                    for n in range(len(heads_of(m, 0))):
                        at = n * (T + 1)
                        for side, where in enumerate((c_bank, m_bank)):
                            h = heads_of(m, side)[n]
                            pe.matmul(where[:, at:at + T + 1], ks[rows(h), h // 2, b * T:b * T + 128],
                                      qs[rows(h), h // 2, cols], start=True, stop=False)
                        for side, where in enumerate((c_bank, m_bank)):
                            h = heads_of(m, side)[n]
                            pe.matmul(where[:, at:at + T + 1], ident_r[0:8, h:h + 1].broadcast_to([8, 128]),
                                      shift_t[:, :], start=False, stop=False)
                        for where in (c_bank, m_bank):
                            last = pe.matmul(where[:, at + 128:at + 146], ident_r[:, :], band_main[:, :],
                                             start=False, stop=True)
                else:
                    for g in range(2):
                        at = g * (T + 1)
                        for r in range(2):
                            pe.matmul(c_bank[:, at:at + T + 1], k_tail[:, 2 * g + r, :], qs[:, 2 * g + r, cols],
                                      start=r == 0, stop=False)
                        pe.matmul(c_bank[:, at:at + T + 1], tail_heads[:, g, :], shift_t[:, :], start=False, stop=False)
                        last = pe.matmul(c_bank[:, at:at + 18], ident_r[:, :], band_tail[:, :], start=False, stop=True)
                pe_c.done(last, f"p{m}_{b}")

            def pv(q, b):
                after(pe, act_c, q, f"p2_{b}")
                for g in range(2):
                    at = g * (T + 1)
                    for j in range(4):
                        h = 4 * g + j
                        pe.matmul(c_bank[:, at:at + T], v_main[:, h * 128:(h + 1) * 128],
                                  prob[:, h * (T + 1):h * (T + 1) + T], start=j == 0, stop=False)
                    last = pe.matmul(c_bank[:, at:at + T], v_tail[:, g, :], prob_tail[:, g, :], start=False, stop=True)
                pe_c.done(last, f"pv{b}")

            def proj(q):
                after(pe, dve_c, q, "on1")
                for g in range(2):
                    last = pe.matmul(c_bank[:, 0:PT], field("proj_w")[:, g * D:(g + 1) * D], o_n[:, g, :],
                                     start=g == 0, stop=g == 1)
                pe_c.done(last, "proj")

            def oht(q):
                after(pe, dve_c, q, "oh")
                for c in range(3):
                    last = pe.matmul(c_bank[0:8, c * 128:(c + 1) * 128], oh_c[:, c, :], ident, start=True, stop=True)
                pe_c.done(last, "oht")

            def up(q, n):
                e, k = n // 2, n % 2
                if n == 0:
                    after(pe, dve_c, q, "oht")
                    after(pe, act_c, q, "back4")
                else:
                    after(pe, act_c, q, f"relu{n - 1}")
                pe.wait_ge(moe_in[e % 4], q * 32 + 16 * (e // 4) + 16)
                pe_c.done(pe.matmul(c_bank[:, 0:PT], moe_w[:, e % 4, k * 128:(k + 1) * 128], xn_c[:, 0:PT],
                                    start=True, stop=True), f"up{n}")

            def down(q, n):
                e, k = n // 2, n % 2
                if n == 0:
                    before(pe, dve_c, q, "moe")
                    after(pe, act_c, q, "oht")
                    pe.matmul(m_bank[:, 0:PT], field("b2", 8), oh_t[:, :], start=True, stop=False)
                after(pe, pool_c, q, f"hm{n}")
                pe_c.done(pe.matmul(m_bank[:, 0:PT], moe_w[:, e % 4, 256 + k * 128:384 + k * 128], hm2[:, n % 2, :],
                                    start=False, stop=n == 2 * E - 1), f"down{n}")

            def emit(q):
                after(pe, act_c, q, f"relu{2 * E - 1}")
                after(pe, dve_c, q, "moe")
                pe_c.done(transposes(chunks(h_c), None, c_bank), "emit")

            ln_a = ln(pe_a, dve_a, h_a, a_bank, {1: "tok", 2: "out"})
            ln_c = ln(pe_c, dve_c, h_c, c_bank, {3: "take", 4: "proj"})
            run(pe, {("A", "tok"): tok, ("A", "ln"): ln_a, ("A", "ln_back"): ln_back(pe_a, dve_a, xt_a, a_bank),
                     ("A", "in"): in_proj, ("A", "wx"): wx, ("A", "tr"): tr, ("A", "mt"): mt_part, ("A", "y"): y,
                     ("A", "out"): out_proj,
                     ("A", "route"): logits(pe_a, act_a, xn_a, "router_w", a_bank, "logits", "back2"),
                     ("A", "owt"): owt, ("A", "bo"): bo,
                     ("B", "gate"): gate_part, ("B", "expert_out"): expert_out,
                     ("C", "ln"): ln_c, ("C", "ln_back"): ln_back(pe_c, dve_c, xt_c, c_bank),
                     ("C", "qk"): qk, ("C", "v"): v, ("C", "smax"): smax, ("C", "shift"): shift,
                     ("C", "prob"): prob_part, ("C", "pv"): pv, ("C", "proj"): proj,
                     ("C", "gate"): logits(pe_c, act_c, xn_c, "gate_w", c_bank, "logits", "back4"),
                     ("C", "oht"): oht, ("C", "up"): up, ("C", "down"): down, ("C", "emit"): emit})

        @block.scalar
        def _(act):
            act.wait_ge(consts_in, 16)
            act.activation(neg_a[:, :], field("a_log", 16), ACT.Exp).then_inc(setup_misc, 1)
            act.wait_ge(setup_misc, 3)
            for n, who in enumerate((act_a, act_b, act_c)):
                act.activation(scrap[:, n:n + 1], field("minus_half")[:, 0:1], ACT.Copy).then_inc(who.sem, len(who.names))

            def back(who, pe_, xn, where):
                def part(q, n):
                    after(act, pe_, q, f"back{n}")
                    if who is act_a:
                        before(act, dve_b, q, "take_lo")
                    who.done(act.activation(xn[:, 0:PT], where[:, 0:PT], ACT.Copy), f"back{n}")
                return part

            def in_part(q, k):
                after(act, pe_a, q, f"in{k}")
                bias = field("in_b")[:, k:k + 1]
                if k < 2:
                    act_a.done(act.activation(conv_in[:, k, :, 3:3 + T], two(a_bank[:, 0:PT]), ACT.Identity,
                                              bias=bias), f"in{k}")
                else:
                    act.activation(gate[:, k - 2, :], a_bank[:, 0:PT], ACT.Identity, bias=bias, scale=0.5)
                    act_a.done(act.activation(th[:, k - 2, :], a_bank[:, 0:PT], ACT.Tanh, bias=bias, scale=0.5),
                               f"in{k}")

            def conv(q):
                after(act, dve_a, q, "conv3")
                after(act, dve_a, q, "silu_res")
                act_a.done(act.activation(th[:, :, :], xc[:, :, :], ACT.Tanh), "th")

            def wx(q):
                after(act, pe_a, q, "wx")
                if not first(q):
                    act.wait_ge(scratch_out, q * 48)
                bias = field("x_b")
                act.activation(b16[:, :], a_bank[0:16, 0:PT], ACT.Identity, bias=bias[0:16])
                act.activation(c16[:, :], a_bank[32:48, 0:PT], ACT.Identity, bias=bias[32:48])
                act_a.done(act.activation(dt16[:, :], a_bank[64:80, 0:PT], ACT.Identity, bias=bias[64:80]), "wx")
                after(act, act_a, q, "wx")
                act_a.done(act.activation(e16[:, :], dt16[:, :], ACT.Abs), "abs")
                after(act, act_a, q, "abs")
                act_a.done(act.activation(e16[:, :], e16[:, :], ACT.Exp, scale=-1.0), "exp")
                after(act, act_a, q, "exp")
                act_a.done(act.activation(e16[:, :], e16[:, :], ACT.Ln, bias=1.0), "ln")

            def scan(q):
                after(act, dve_a, q, "cum")
                act.activation(e16[:, :], dt16[:, :], ACT.Exp)
                act_a.done(act.activation(s16[:, :], dt16[:, :], ACT.Exp, scale=-1.0), "p")

            def tr(q, b):
                after(act, pe_a, q, f"tr{b}")
                act.activation(xc_t[:, 0:256], a_bank[:, 0:256], ACT.Copy)
                act_a.done(act.activation(xc_t[0:TAIL, 256:512], a_bank[0:TAIL, 256:512], ACT.Copy), f"tr{b}")

            def route(q):
                after(act, dve_a, q, "gap")
                act_a.done(act.activation(e_gap[:, :], e_gap[:, :], ACT.Exp), "e_gap")

            def owt(q):
                after(act, pe_a, q, "owt")
                act_a.done(act.activation(ow_t[:, :], a_bank[0:26, 0:PT], ACT.Copy), "owt")

            def gate_part(q, u, g):
                e = u % E
                after(act, pe_b, q, f"{GATES[g]}{u}")
                if g == 0:
                    if u:
                        after(act, dve_b, q, f"c{u - 1}")
                    else:
                        before(act, dve_b, q, f"c{PAIR_UNITS - 1}")
                if g == 3 and u == 0:
                    before(act, dve_b, q, f"h{PAIR_UNITS - 1}")
                if g == 3 and u:
                    after(act, dve_b, q, f"h{u - 1}")
                act_b.done(act.activation(act4[:, g, :], gates[g][:, 0:PT], ACT.Tanh,
                                          bias=field("lstm_b")[:, 4 * e + g:4 * e + g + 1],
                                          scale=1.0 if g == 2 else 0.5), f"{GATES[g]}{u}")

            def tanh_c(q, u):
                after(act, dve_b, q, f"c{u}")
                if u:
                    after(act, dve_b, q, f"hm{u - 1}")
                else:
                    before(act, dve_b, q, f"hm{PAIR_UNITS - 1}")
                act_b.done(act.activation(hid2[:, :], cell2[:, u % E, :], ACT.Tanh, scale=0.5), f"tc{u}")

            def qk(q, w, p):
                after(act, pe_c, q, f"{w}{p}")
                act_c.done(act.activation(qk_hi[:, :], c_bank[:, 0:PT], ACT.Copy), f"{w}{p}")

            def v(q, b):
                after(act, pe_c, q, f"v{b}")
                dst = bass.AP(v_main[:, :].tensor, 0, [[NH * 128, 128], [512, 2], [128 + 32, 4], [1, HD]])
                act_c.done(act.activation(dst, c_bank[:, 0:128].rearrange("p (g j d) -> p g j d", g=2, j=4), ACT.Copy),
                           f"v{b}")

            def shift(q, b):
                after(act, pe_c, q, f"shift{b}")
                act_c.done(act.activation(shift_t[:, :], c_bank[0:8, 0:T + 1], ACT.Copy, scale=-1.0), f"shift{b}")

            def prob_part(q, b, m):
                after(act, pe_c, q, f"p{m}_{b}")
                if (b, m) == (0, 0):
                    before(act, pool_c, q, f"hm{2 * E - 1}")
                scale = float(D) ** -0.5
                if m < 2:
                    for side, where in enumerate((c_bank, m_bank)):
                        hs = heads_of(m, side)
                        dst = prob[:, :].rearrange("p (h t) -> p h t", t=T + 1)[:, hs[0]:hs[-1] + 1:2, 0:T]
                        ins = act.activation(dst, per_head(where, len(hs)), ACT.Exp, scale=scale)
                else:
                    ins = act.activation(prob_tail[:, :, :], per_head(c_bank, 2), ACT.Exp, scale=scale)
                act_c.done(ins, f"p{m}_{b}")

            def oht(q):
                after(act, pe_c, q, "oht")
                act_c.done(act.activation(oh_t[:, :], c_bank[0:8, 0:PT], ACT.Copy), "oht")

            def up(q, n):
                after(act, pe_c, q, f"up{n}")
                if n >= 2:
                    after(act, pool_c, q, f"hm{n - 2}")
                act_c.done(act.activation(relu2[:, n % 2, :], c_bank[:, 0:PT], ACT.Relu,
                                          bias=field("w1_b")[:, n:n + 1]), f"relu{n}")

            def emit(q):
                after(act, pe_c, q, "emit")
                act_c.done(act.activation(out_sb[:, :, :].rearrange("p c d -> p (c d)"), c_bank[:, 0:PAD], ACT.Copy), "emit")

            run(act, {("A", "ln_back"): back(act_a, pe_a, xn_a, a_bank), ("A", "in"): in_part, ("A", "conv"): conv,
                      ("A", "wx"): wx, ("A", "scan"): scan, ("A", "tr"): tr, ("A", "route"): route, ("A", "owt"): owt,
                      ("B", "gate"): gate_part, ("B", "tanh_c"): tanh_c,
                      ("C", "ln_back"): back(act_c, pe_c, xn_c, c_bank), ("C", "qk"): qk, ("C", "v"): v,
                      ("C", "shift"): shift, ("C", "prob"): prob_part, ("C", "oht"): oht, ("C", "up"): up,
                      ("C", "emit"): emit})

        @block.gpsimd
        def _(pool):
            pool.wait_ge(consts_in, 16)
            pool.wait_ge(setup_misc, 3)
            for n, who in enumerate((pool_a, pool_b, pool_c)):
                pool.memset(scrap[:, 3 + n:4 + n], 0.0).then_inc(who.sem, len(who.names))

            def ln(who, dve, mv_, ve_, rstd_):
                def part(q, n):
                    after(pool, dve, q, f"ln{n}_mv")
                    plain(pool)
                    who.done(pool.tensor_scalar(ve_[:, :], mv_[:, :, 1], LN_EPS, None, ALU.add), f"ve{n}")
                    after(pool, who, q, f"ve{n}")
                    who.done(pool.tensor_tensor(rstd_[:, :], ve_[:, :], field("minus_half"), ALU.pow), f"rstd{n}")
                return part

            def mask_x(q, u):
                b, e = u // E, u % E
                if u >= 2:
                    after(pool, pe_b, q, f"o{u - 2}")
                else:
                    before(pool, pe_b, q, f"o{u + PAIR_UNITS - 2}")
                if u == 0:
                    after(pool, dve_b, q, "take_lo")
                hs = u // 4
                if u % 4 == 0:
                    pool.wait_ge(onehot_in[hs % 2], q * 32 + 16 * (hs // 2) + 16)
                mask = onehot[hs % 2][:, e % 4, :, :]
                pool.tensor_tensor(two(mx_hi[:, u % 2, :]), spread(xb_hi[:, b * T:b * T + T], 1, 2), mask, ALU.mult)
                pool_b.done(pool.tensor_tensor(two(mx_lo[:, u % 2, :]), spread(xb_lo[:, b * T:b * T + T], 1, 2), mask,
                                               ALU.mult), f"mx{u}")

            def tails(q, b):
                after(pool, dve_c, q, "k3")
                if b:
                    after(pool, pe_c, q, "p2_0")
                else:
                    before(pool, pe_c, q, "p2_1")
                own = spread(field("own_cols").rearrange("p (a j) -> p a j", a=4), 3, TAIL)
                for dst, src, name in ((q_tail, qs, "qt"), (k_tail, ks, "kt")):
                    pool_c.done(pool.tensor_tensor(
                        dst[:, :, :].rearrange("p a (j i) -> p a j i", j=4)[:, :, :, 0:TAIL],
                        spread(src[:, :, b * T + 128:b * T + T], 2, 4), own, ALU.mult), f"{name}{b}")

            def mask_h(q, n):
                after(pool, act_c, q, f"relu{n}")
                if n == 0:
                    pool.wait_ge(onehot_c_in, q * 16 + 16)
                if n >= 2:
                    after(pool, pe_c, q, f"down{n - 2}")
                pool_c.done(pool.tensor_tensor(hm2[:, n % 2, :], relu2[:, n % 2, :], onehot_c[:, n // 2, :], ALU.mult),
                            f"hm{n}")

            run(pool, {("A", "ln"): ln(pool_a, dve_a, mv, ve, rstd), ("B", "mask_x"): mask_x,
                       ("C", "ln"): ln(pool_c, dve_c, mv_c, ve_c, rstd_c), ("C", "v"): tails, ("C", "up"): mask_h})

        @block.vector
        def _(dve):
            for tile in (h_a, xn_a, h_c, xn_c):
                dve.memset(tile[:, PT:PAD], 0.0)
            for tile in (hh, hl, q_tail, k_tail):
                dve.memset(tile[:, :, :].bitcast(F32), 0.0)
            for tile in (qs, ks):
                dve.memset(tile[:, :, PT:PT + 2].bitcast(F32), 0.0)
            dve.memset(conv_in[:, :, :, 0:3], 0.0)
            dve.wait_ge(consts_in, 16)
            dve.wait_ge(once_in, 16)
            dve.tensor_copy(ident_r[:, :], ident)
            dve.tensor_copy(band_main[:, :], once_field("band_main"))
            dve.tensor_copy(band_tail[:, :], once_field("band_tail"))
            dve.tensor_copy(tail_heads[:, :, :].rearrange("p g c -> p (g c)"), once_field("tail_heads", 8))
            for name, cols in (("lstm_out_w", slice(None)), ("conv_w", slice(None)), ("conv_b", slice(None)),
                               ("in_b", slice(2, 4))):
                dve.tensor_scalar(field(name)[:, cols], field(name)[:, cols], 0.5, None, ALU.mult)
            for g in (0, 1, 3):
                bias = field("lstm_b").rearrange("p (e g) -> p g e", g=4)[:, g, :]
                dve.tensor_scalar(bias, bias, 0.5, None, ALU.mult)
            dve.tensor_copy(h_add[:, 0:1], once_field("cls_a"))
            dve.tensor_tensor(h_add[:, 1:2], once_field("cls_b"), once_field("pos")[:, 0:1], ALU.add)
            dve.tensor_scalar(h_add[:, 2:T], once_field("pos")[:, 1:T - 1], once_field("tok_b"), None, ALU.add)
            dve.wait_ge(setup_misc, 1)
            dve.tensor_scalar(neg_a[:, :], neg_a[:, :], -1.0, None, ALU.mult)
            stage = cell2[:, :, :].rearrange("p e t -> p (e t)")
            for c in range(8):
                hi, lo = (wh_hi, wh_lo) if c < 4 else (wi_hi, wi_lo)
                cols, src = slice((c % 4) * 1024, (c % 4 + 1) * 1024), stage[:, (c % 2) * 1024:(c % 2 + 1) * 1024]
                scale = 0.5 if c < 4 else 1.0
                dve.wait_ge(stage_in[c % 2], 16 * (c // 2) + 16)
                dve.tensor_scalar(hi[:, cols], src, scale, None, ALU.mult).then_inc(setup_split, 1)
                dve.wait_ge(setup_split, c + 1)
                dve.scalar_tensor_tensor(lo[:, cols], src, scale, hi[:, cols], ALU.mult, ALU.subtract
                                         ).then_inc(split_done, 1)
            dve.wait_ge(split_done, 8)
            dve.memset(cell2[:, :, :], 0.0).then_inc(setup_misc, 2)
            dve.wait_ge(setup_misc, 3)
            for n, who in enumerate((dve_a, dve_b, dve_c)):
                dve.memset(scrap[:, 6 + n:7 + n], 0.0).then_inc(who.sem, len(who.names))

            def tok(q):
                after(dve, pe_a, q, "tok")
                dve_a.done(dve.tensor_tensor(two(h_a[:, 0:PT]), two(a_bank[:, 0:PT]), spread(h_add[:, :], 1, 2), ALU.add),
                           "tok")

            def ln(who, pe_, pool_, where, stats_, mv_, rstd_, xt):
                def part(q, n):
                    after(dve, pe_, q, f"ln{n}")
                    for c in range(3):
                        ins = dve.bn_stats(stats_[:, c, :], where[:, c * 128:(c + 1) * 128])
                    who.done(ins, f"ln{n}_s")
                    after(dve, who, q, f"ln{n}_s")
                    plain(dve)
                    for c in range(3):
                        ins = dve.bn_aggr(mv_[:, c, :], stats_[:, c, :])
                    who.done(ins, f"ln{n}_mv")
                return part

            def ln_x(who, pool_, where, mv_, rstd_, xt):
                def part(q, n):
                    after(dve, who, q, f"ln{n}_mv")
                    after(dve, pool_, q, f"rstd{n}")
                    for c in range(3):
                        ins = dve.tensor_scalar(xt[:, c, :], where[:, c * 128:(c + 1) * 128], mv_[:, c, 0:1],
                                                rstd_[:, c:c + 1], ALU.subtract, ALU.mult)
                    who.done(ins, f"ln{n}_x")
                return part

            def silu_res(q, k):
                if k == 3:
                    after(dve, act_a, q, "in3")
                    dve_a.done(dve.scalar_tensor_tensor(gate[:, :, :], th[:, :, :], 1.0, gate[:, :, :], ALU.add, ALU.mult),
                               "silu_res")

            def conv(q):
                after(dve, act_a, q, "in1")
                for j in range(4):
                    if j:
                        after(dve, dve_a, q, f"conv{j - 1}")
                    for k in range(2):
                        w = field("conv_w")[:, 4 * k + j:4 * k + j + 1]
                        src, dst = conv_in[:, k, :, j:j + T], two(xc[:, k, :])
                        if j == 0:
                            ins = dve.tensor_scalar(dst, src, w, field("conv_b")[:, k:k + 1], ALU.mult, ALU.add)
                        else:
                            ins = dve.scalar_tensor_tensor(dst, src, w, dst, ALU.mult, ALU.add)
                    dve_a.done(ins, f"conv{j}")
                after(dve, act_a, q, "th")
                dve_a.done(dve.scalar_tensor_tensor(xc[:, :, :], th[:, :, :], 1.0, xc[:, :, :], ALU.add, ALU.mult), "xc")

            def scan(q):
                after(dve, act_a, q, "ln")
                dve_a.done(dve.scalar_tensor_tensor(dt16[:, :], dt16[:, :], 0.0, e16[:, :], ALU.max, ALU.add), "dt")
                after(dve, dve_a, q, "dt")
                for b in range(2):
                    cols = slice(b * T, b * T + T)
                    ins = dve.tensor_tensor_scan(s16[:, cols], dt16[:, cols], dt16[:, cols], 0.0, ALU.add, ALU.bypass)
                dve_a.done(ins, "sum")
                after(dve, dve_a, q, "sum")
                dve_a.done(dve.tensor_scalar(dt16[:, :], s16[:, :], neg_a[:, :], CUM_EPS_LOG, ALU.mult, ALU.max), "cum")
                after(dve, act_a, q, "p")
                dve.tensor_tensor(c16[:, :], c16[:, :], e16[:, :], ALU.mult)
                dve_a.done(dve.tensor_tensor(b16[:, :], b16[:, :], s16[:, :], ALU.mult), "qk")

            def mt_part(q, b):
                after(dve, pe_a, q, f"mt{b}")
                dve.tensor_tensor(mt[:, 0:T], a_bank[:, 0:T], field("causal"), ALU.mult)
                dve_a.done(dve.tensor_tensor(mt[0:TAIL, T:T + TAIL], a_bank[0:TAIL, T:T + TAIL],
                                             field("causal", TAIL)[:, 0:TAIL], ALU.mult), f"mt{b}")

            def y(q, b):
                after(dve, pe_a, q, f"y{b}")
                cols = slice(b * T, b * T + T)
                for k in range(2):
                    ins = dve.scalar_tensor_tensor(th[:, k, cols], xc[:, k, cols], field("skip_d")[:, k:k + 1],
                                                   a_bank[:, k * T:k * T + T], ALU.mult, ALU.add)
                dve_a.done(ins, f"y{b}")
                after(dve, dve_a, q, f"y{b}")
                dve_a.done(dve.tensor_tensor(gate[:, :, cols], th[:, :, cols], gate[:, :, cols], ALU.mult), f"yg{b}")

            def out_proj(q):
                after(dve, pe_a, q, "out")
                dve_a.done(dve.scalar_tensor_tensor(h_a[:, 0:PT], a_bank[:, 0:PT], field("out_b"), h_a[:, 0:PT],
                                                    ALU.add, ALU.add), "out")

            def top8(who, pe_, where, bias, lg_, top_, top_i_, tag):
                def part(q):
                    after(dve, pe_, q, "logits")
                    who.done(dve.tensor_tensor(lg_[:, :, :], where[:, 0:24].rearrange("p (c e) -> p c e", c=3),
                                               spread(field(bias), 1, 3), ALU.add), "lg")
                    after(dve, who, q, "lg")
                    plain(dve)
                    for c in range(3):
                        ins = dve.max(top_[:, c, :], lg_[:, c, :])
                    who.done(ins, "top")
                    after(dve, who, q, "top")
                    plain(dve)
                    for c in range(3):
                        ins = dve.max_index(top_i_[:, c, :], top_[:, c, :], lg_[:, c, :])
                    who.done(ins, "top_i")
                    after(dve, who, q, "top_i")
                return part

            top_a = top8(dve_a, pe_a, a_bank, "router_b", lg, top, top_i, "a")
            top_cc = top8(dve_c, pe_c, c_bank, "gate_b", lg_c, top_c, top_ic, "c")

            def route(q):
                top_a(q)
                dve.tensor_copy(top_f[:, :, :], top_i[:, :, 0:2])
                dve_a.done(dve.tensor_tensor(e_gap[:, :], top[:, :, 1], top[:, :, 0], ALU.subtract), "gap")
                after(dve, dve_a, q, "gap")
                hot = ow[:, :, 8:24].rearrange("p c (k e) -> p c k e", k=2)
                for c in range(3):
                    dve.tensor_tensor(hot[:, c, :, :], spread(field("iota"), 1, 2), spread(top_f[:, c, :], 2, E), ALU.is_equal)
                after(dve, act_a, q, "e_gap")
                dve_a.done(dve.tensor_scalar(e_sum[:, :], e_gap[:, :], 1.0, None, ALU.add), "e_sum")
                after(dve, dve_a, q, "e_sum")
                dve_a.done(dve.reciprocal(ow[:, :, 24], e_sum[:, :]), "w0")
                after(dve, dve_a, q, "w0")
                dve_a.done(dve.tensor_tensor(ow[:, :, 25], e_gap[:, :], ow[:, :, 24], ALU.mult), "w1")
                after(dve, dve_a, q, "w1")
                dve.tensor_tensor(ow_w[:, :, :], ow[:, :, 8:16], ow[:, :, 24:25].broadcast_to([128, 3, 8]), ALU.mult)
                dve_a.done(dve.tensor_tensor(ow[:, :, 0:8], ow[:, :, 16:24], ow[:, :, 25:26].broadcast_to([128, 3, 8]),
                                             ALU.mult), "ow1")
                after(dve, dve_a, q, "ow1")
                dve_a.done(dve.tensor_tensor(ow[:, :, 0:8], ow[:, :, 0:8], ow_w[:, :, :], ALU.add), "ow")

            def owt(q):
                after(dve, act_a, q, "owt")
                dve_a.done(dve.tensor_copy(ow_b[:, :], a_bank[0:24, 0:PT]), "owt")

            def bo(q):
                after(dve, pe_a, q, "bo")
                dve_a.done(dve.tensor_tensor(h_a[:, 0:PT], h_a[:, 0:PT], a_bank[:, 0:PT], ALU.add), "bo")

            def take_b(q):
                after(dve, dve_a, q, "bo")
                before(dve, dve_b, q, "h2_1")
                dve.tensor_copy(h1[:, :], h_a[:, 0:PT])
                after(dve, act_a, q, "back2")
                before(dve, pool_b, q, f"mx{PAIR_UNITS - 1}")
                dve_b.done(dve.tensor_copy(xb_hi[:, :], xn_a[:, 0:PT]), "take_hi")
                after(dve, dve_b, q, "take_hi")
                dve_b.done(dve.tensor_tensor(xb_lo[:, :], xn_a[:, 0:PT], xb_hi[:, :], ALU.subtract), "take_lo")

            def cell(q, u):
                e = u % E
                after(dve, act_b, q, f"i{u}")
                dve.scalar_tensor_tensor(act4[:, 0, :], act4[:, 0, :], 1.0, cell2[:, e, :], ALU.add, ALU.mult)
                after(dve, act_b, q, f"g{u}")
                dve_b.done(dve.scalar_tensor_tensor(act4[:, 2, :], act4[:, 1, :], 1.0, act4[:, 2, :], ALU.add, ALU.mult),
                           f"ig{u}")
                after(dve, dve_b, q, f"ig{u}")
                dve_b.done(dve.scalar_tensor_tensor(cell2[:, e, :], act4[:, 0, :], 0.5, act4[:, 2, :], ALU.mult, ALU.add),
                           f"c{u}")

            def hidden(q, u):
                e = u % E
                after(dve, act_b, q, f"tc{u}")
                dve_b.done(dve.scalar_tensor_tensor(hid2[:, :], act4[:, 3, :], 1.0, hid2[:, :], ALU.add, ALU.mult), f"h{u}")
                after(dve, dve_b, q, f"h{u}")
                dve_b.done(dve.tensor_copy(hh[:, e, :], hid2[:, :]), f"hh{u}")
                if u:
                    after(dve, pe_b, q, f"z{u - 1}")
                else:
                    before(dve, pe_b, q, f"z{PAIR_UNITS - 1}")
                hs = u // 4
                if u % 4 == 0:
                    dve.wait_ge(onehot_in[hs % 2], q * 32 + 16 * (hs // 2) + 16)
                dve_b.done(dve.tensor_tensor(two(hm[:, :]), two(hid2[:, :]), onehot[hs % 2][:, e % 4, :, :], ALU.mult),
                           f"hm{u}")
                after(dve, dve_b, q, f"hh{u}")
                dve_b.done(dve.tensor_tensor(hl[:, e, :], hid2[:, :], hh[:, e, :], ALU.subtract), f"hl{u}")

            def step_out(q, b):
                after(dve, pe_b, q, f"z{E * b + E - 1}")
                dve.wait_ge(slot_w_in[b], q * 16 + 16)
                dve_b.done(dve.tensor_tensor(z_tmp[:, :, :], two(z_bank[:, 0:PT]), slot_w[b][:, :, :], ALU.mult), f"zz{b}")
                after(dve, dve_b, q, f"zz{b}")
                cols = slice(b * T, b * T + T)
                dve_b.done(dve.tensor_tensor(z_tmp[:, 0, :], z_tmp[:, 0, :], z_tmp[:, 1, :], ALU.add), f"sum{b}")
                after(dve, dve_b, q, f"sum{b}")
                dve_b.done(dve.tensor_tensor(h2[:, cols], h1[:, cols], z_tmp[:, 0, :], ALU.add), f"h2_{b}")

            def take_c(q):
                after(dve, dve_b, q, "h2_1")
                before(dve, pe_c, q, "emit")
                dve_c.done(dve.tensor_copy(h_c[:, 0:PT], h2[:, :]), "take")

            def qk(q, w, p):
                after(dve, act_c, q, f"{w}{p}")
                dst = (qs if w == "q" else ks)[:, p, 0:PT]
                dve_c.done(dve.scalar_tensor_tensor(dst, qk_hi[:, :], field(f"{w}_lo"), c_bank[:, 0:PT], ALU.mult, ALU.add),
                           f"{w}{p}")

            def v(q, b):
                after(dve, act_c, q, f"v{b}")
                own = spread(spread(field("own_row"), 1, 2), 3, HD)
                dve_c.done(dve.tensor_tensor(v_tail[:, :, :].rearrange("p g (j d) -> p g j d", j=4)[:, :, :, 0:HD],
                                             c_bank[:, 128:256].rearrange("p (g j d) -> p g j d", g=2, j=4), own, ALU.mult),
                           f"v{b}")

            def smax(q, b, m):
                after(dve, pe_c, q, f"s{m}_{b}")
                if m < 2:
                    for side, where in enumerate((c_bank, m_bank)):
                        hs = heads_of(m, side)
                        ins = dve.tensor_reduce(row_max[:, hs[0]:hs[-1] + 1:2], per_head(where, len(hs)), AX.X, ALU.max)
                else:
                    ins = dve.tensor_reduce(tail_max[:, :], per_head(c_bank, 2), AX.X, ALU.max)
                dve_c.done(ins, f"s{m}_{b}")
                if m == 2:
                    after(dve, dve_c, q, f"s2_{b}")
                    dve_c.done(dve.tensor_tensor(tail_max_own[:, :, :], spread(tail_max[:, :], 2, 4),
                                                 spread(field("own_row"), 1, 2), ALU.mult), f"own_{b}")

            def pv(q, b):
                after(dve, pe_c, q, f"pv{b}")
                plain(dve)
                src = c_bank[:, 0:2 * (T + 1)].rearrange("p (g t) -> p g t", t=T + 1)[:, :, 0:T]
                cols = slice(b * T, b * T + T)
                dve_c.done(dve.stream_shuffle(norm[:, :, cols], src, [HD + i % HD for i in range(32)]), f"den{b}")
                after(dve, dve_c, q, f"den{b}")
                dve_c.done(dve.reciprocal(norm[:, :, cols], norm[:, :, cols]), f"inv{b}")
                after(dve, dve_c, q, f"inv{b}")
                dve_c.done(dve.tensor_tensor(o_n[:, :, cols], src, norm[:, :, cols], ALU.mult), f"on{b}")

            def proj(q):
                after(dve, pe_c, q, "proj")
                dve_c.done(dve.tensor_tensor(h_c[:, 0:PT], h_c[:, 0:PT], c_bank[:, 0:PT], ALU.add), "proj")

            def moe_gate(q):
                top_cc(q)
                dve_c.done(dve.tensor_copy(top_fc[:, :, :], top_ic[:, :, 0:1]), "top_f")
                after(dve, dve_c, q, "top_f")
                dve_c.done(dve.tensor_tensor(oh_c[:, :, :], spread(field("iota"), 1, 3),
                                             top_fc[:, :, 0:1].broadcast_to([128, 3, E]), ALU.is_equal), "oh")

            def oht(q):
                after(dve, act_c, q, "oht")
                dve_c.done(dve.tensor_copy(oh_b[:, :], c_bank[0:8, 0:PT]), "oht")

            def emit(q):
                after(dve, pe_c, q, f"down{2 * E - 1}")
                dve_c.done(dve.tensor_tensor(h_c[:, 0:PT], h_c[:, 0:PT], m_bank[:, 0:PT], ALU.add), "moe")

            ln_args_a = (dve_a, pe_a, pool_a, a_bank, stats, mv, rstd, xt_a)
            ln_args_c = (dve_c, pe_c, pool_c, c_bank, stats_c, mv_c, rstd_c, xt_c)
            run(dve, {("A", "tok"): tok, ("A", "ln"): ln(*ln_args_a),
                      ("A", "ln_back"): ln_x(dve_a, pool_a, a_bank, mv, rstd, xt_a),
                      ("A", "in"): silu_res, ("A", "conv"): conv, ("A", "scan"): scan, ("A", "mt"): mt_part,
                      ("A", "y"): y, ("A", "out"): out_proj, ("A", "route"): route, ("A", "owt"): owt, ("A", "bo"): bo,
                      ("B", "take"): take_b, ("B", "cell"): cell, ("B", "hidden"): hidden, ("B", "step_out"): step_out,
                      ("C", "take"): take_c, ("C", "ln"): ln(*ln_args_c),
                      ("C", "ln_back"): ln_x(dve_c, pool_c, c_bank, mv_c, rstd_c, xt_c), ("C", "qk"): qk, ("C", "v"): v,
                      ("C", "smax"): smax, ("C", "pv"): pv, ("C", "proj"): proj, ("C", "gate"): moe_gate,
                      ("C", "oht"): oht, ("C", "emit"): emit})


def _layout(inputs):
    f = {k: np.asarray(v) for k, v in inputs.items()}
    x = f["x"]
    nb = x.shape[0]
    npairs = nb // 2
    patches = x.reshape(nb, 3, 11, 16, 13, 16).transpose(3, 5, 1, 0, 2, 4).reshape(KC, D, npairs, 2, T - 2)
    x_t = np.zeros((npairs + 1, D, KC, 2, T), np.float32)
    x_t[:npairs, :, :, :, 2:] = patches.transpose(2, 1, 0, 3, 4)
    x_t = x_t.reshape(npairs + 1, D, KC, PT)

    order = [1, 0, 2, 3]
    def gates_first(w):
        return w.reshape(E, D, 4, D)[:, :, order].transpose(1, 0, 2, 3).reshape(D, E * 4 * D)

    p = {name: np.zeros((128, n), np.float32) for name, n in {**FIELDS, **ONCE}.items()}
    p["tok_w"][:] = f["L0_tok_W"].reshape(D, KC, 128).transpose(2, 1, 0).reshape(128, KC * D)
    p["in_w"][:] = f["L0_attn_W_in"]
    x_w = f["L0_attn_W_x"].reshape(2, 128, 2 * DS + 1).transpose(1, 0, 2)
    wx = p["x_w"].reshape(128, 2, 80)
    wx[:, :, 0:DS], wx[:, :, 32:32 + DS], wx[:, :, 64:64 + DS] = x_w[:, :, :DS], x_w[:, :, DS:2 * DS], x_w[:, :, 2 * DS:]
    p["x_b"][0:DS, 0], p["x_b"][32:32 + DS, 0] = f["L0_attn_b_x"][:DS], f["L0_attn_b_x"][DS:2 * DS]
    p["x_b"][64:64 + DS, 0] = f["L0_attn_b_x"][2 * DS]
    p["a_log"][0:DS, 0] = f["L0_attn_A_log"]
    p["out_w"][:] = f["L0_attn_W_out"].reshape(2, 128, D).transpose(1, 0, 2).reshape(128, 2 * D)
    p["out_b"][:, 0] = f["L0_attn_b_out"]
    p["in_b"][:] = f["L0_attn_b_in"].reshape(4, 128).T
    p["conv_w"][:] = f["L0_attn_conv_w"].reshape(2, 128, 4).transpose(1, 0, 2).reshape(128, 8)
    p["conv_b"][:] = f["L0_attn_conv_b"].reshape(2, 128).T
    p["skip_d"][:] = f["L0_attn_D"].reshape(2, 128).T
    p["tok_b"][:, 0] = f["L0_tok_b"]
    p["cls_a"][:, 0], p["cls_b"][:, 0] = f["cls_tok"].reshape(D), f["L0_tok_cls_token"].reshape(D)
    p["pos"][:] = f["L0_tok_pos_emb"].reshape(1, T - 1)
    p["lstm_out_w"][:] = f["L0_ffn_Wo"].transpose(1, 0, 2).reshape(128, E * D)
    p["lstm_b"][:] = f["L0_ffn_b"].reshape(E, 4, D)[:, order].transpose(2, 0, 1).reshape(128, 4 * E)
    p["router_w"][:], p["router_b"][:] = f["L0_ffn_router_w"], f["L0_ffn_router_b"]
    p["gate_w"][:], p["gate_b"][:] = f["L1_ffn_Wg"], f["L1_ffn_bg"]
    p["bo"][0:E], p["b2"][0:E] = f["L0_ffn_bo"], f["L1_ffn_b2"]
    p["w1_b"][:] = f["L1_ffn_b1"].reshape(2 * E, 128).T
    qkv = f["L1_attn_w_qkv"].reshape(D, NH, 3, HD)
    for name, part in (("q_w", 0), ("k_w", 1)):
        p[name].reshape(D, NH, 4, HD)[:, :, 0:3] = qkv[:, :, part][:, :, None]
    p["v_w"][:] = qkv[:, :, 2].reshape(D, D)
    p["q_lo"].reshape(2, 4, 16)[:, 2] = -1.0
    p["k_lo"].reshape(2, 4, 16)[:, 1] = -1.0
    p["proj_w"].reshape(4, 32, 2, D)[:, 0:HD] = f["L1_attn_w_proj"].reshape(2, 4, HD, D).transpose(1, 2, 0, 3)

    row, col = np.arange(128)[:, None], np.arange(T)[None]
    p["ident"][:] = np.eye(128)
    p["causal"][:] = col >= row
    p["band_main"][:] = np.where(128 + col[:, :18] - row > 128, -1e9, 0.0)
    p["band_tail"][:] = np.where((128 + row % 32) - col[:, :18] > 128, -1e9, 0.0)
    pair_, j = np.arange(4)[:, None], np.arange(4)[None]
    p["own_cols"][:] = (j == 2 * (pair_ % 2) + row[:, :, None] // 64).reshape(128, 16)
    p["own_row"][:] = (j == row // 32) & (row % 32 < TAIL)
    p["tail_sel"][:] = (row % 32 == col[:, :18]) & (col[:, :18] < TAIL)
    p["iota"][:] = np.arange(E)
    p["minus_half"][:] = -0.5
    heads = p["tail_heads"].reshape(128, 2, 4, 32)
    for h in range(NH):
        heads[h, h // 4, h % 4, 0:TAIL] = 1.0
    packed, once = (np.concatenate([p[name] for name in names], axis=1) for names in (FIELDS, ONCE))

    v_ones = np.zeros((128, 1280), np.float32)
    for h in range(NH):
        v_ones[:, h * 128 + 32 * (h % 4) + HD:h * 128 + 32 * (h % 4) + 2 * HD] = 1.0
    v_ones[:, 1024:].reshape(128, 2, 4, 2, HD)[:, :, :, 1] = p["own_row"][:, None, :, None]
    w1 = f["L1_ffn_W1"]
    w2 = f["L1_ffn_W2"].reshape(E, 2, 128, D).transpose(0, 2, 1, 3).reshape(E, 128, 2 * D)
    return {"x_t": x_t, "wh": gates_first(f["L0_ffn_Wh"]), "wi": gates_first(f["L0_ffn_Wi"]),
            "wmoe": np.concatenate([w1, w2], axis=2), "packed": packed, "once": once, "v_ones": v_ones}


def _program(nc, arrays, nb):
    args = {}
    for name, a in arrays.items():
        args[name] = nc.dram_tensor(f"in_{name}", a.shape, mybir.dt.from_np(a.dtype), kind="ExternalInput").ap()
    args["out"] = nc.dram_tensor("out_0", (nb * T, D), F32, kind="ExternalOutput").ap()
    args["scr_onehot"] = nc.dram_tensor("scr_onehot", (2, E, 2, T), BF16).ap()
    args["scr_weight"] = nc.dram_tensor("scr_weight", (2, 2, T), F32).ap()
    args["scr_moe"] = nc.dram_tensor("scr_moe", (E, PT), BF16).ap()
    build(nc, **args)


def kernel(**inputs):
    import concourse.bacc as bacc
    from concourse.bass_utils import run_bass_kernel_spmd
    arrays = {k: np.ascontiguousarray(a) for k, a in _layout(inputs).items()}
    nb = np.asarray(inputs["x"]).shape[0]
    nc = bacc.Bacc("TRN2", target_bir_lowering=False, num_devices=1)
    _program(nc, arrays, nb)
    r = run_bass_kernel_spmd(nc, [{f"in_{k}": a for k, a in arrays.items()}], core_ids=[0])
    return r.results[0]["out_0"].reshape(nb, T, D)
```

```python
from contextlib import ExitStack

import numpy as np
import concourse.bass as bass
from concourse import mybir

F32, R32, BF16, U32 = mybir.dt.float32, mybir.dt.float32r, mybir.dt.bfloat16, mybir.dt.uint32
ALU, ACT, AX = mybir.AluOpType, mybir.ActivationFunctionType, mybir.AxisListType

D, T = 128, 145
PT = 2 * T
PAD = 384
TAIL = T - 128
E, NH, HD = 8, 8, 16
DS = 16
KC = 6
PAIR_UNITS = 16
LN_EPS = 1e-5
CUM_EPS_LOG = float(np.log(1e-8))
GATES = ("f", "i", "g", "o")
REST = {"take": 0.3, "ln": 2.5, "ln_x": 0.5, "ln_back": 1, "qk": 1, "v": 1, "smax": 1.25, "shift": 2.3, "prob": 2.6,
        "pv": 1.9, "proj": 1, "gate": 2.1, "oht": 1, "up": 0.5, "down": 0.5, "emit": 0, "tok": 1, "in": 0.98,
        "conv": 1, "silu": 0.35, "xc": 0.5, "softplus": 0.6, "exps": 0.5, "cb": 0.5, "weights": 2, "wx": 1,
        "scan": 1.4, "tr": 2, "mt": 1, "y": 4.2, "out": 0.7, "route": 1.4, "owt": 0.3, "bo": 0, "scratch": 0}
NUDGE = {("C", "down", 4): -1, ("C", "down", 3): -3, ("C", "shift", 1): 3, ("C", "down", 2): 2, ("C", "down", 0): -1,
         ("A", "route"): 1, ("A", "scratch"): -3}
LAG = {"mask_x": 0, "cell": 3, "tanh_c": 4, "hidden": 5, "expert_out": 8, "masks": 11}
A_LEAD = 13
STEP_NAMES = {
    "pe_a": (
        "tok ln1 back1 in0 in1 in2 in3 wx tr0 mt0 y0 tr1 mt1 y1 out ln2 back2 logits owt bo "
    ).split(),
    "pe_b": (
        "f0 i0 g0 o0 f1 i1 g1 o1 f2 z0 i2 g2 o2 f3 z1 i3 g3 o3 f4 z2 i4 g4 o4 f5 z3 i5 g5 o5 f6 z4 i6 g6 o6 "
        "f7 z5 i7 g7 o7 f8 z6 i8 g8 o8 f9 z7 i9 g9 o9 f10 z8 i10 g10 o10 f11 z9 i11 g11 o11 f12 z10 i12 g12 "
        "o12 f13 z11 i13 g13 o13 f14 z12 i14 g14 o14 f15 z13 i15 g15 o15 z14 z15 "
    ).split(),
    "pe_c": (
        "ln3 back3 q0 q1 q2 q3 k0 k1 k2 k3 v0 s0_0 s1_0 shift0 p0_0 p1_0 pv0 v1 s0_1 s1_1 shift1 p0_1 p1_1 "
        "pv1 proj ln4 back4 logits oht up0 up1 down0 up2 down1 up3 down2 up4 down3 up5 down4 up6 down5 up7 "
        "down6 up8 down7 up9 down8 up10 down9 up11 down10 up12 down11 up13 down12 up14 down13 up15 down14 "
        "down15 emit "
    ).split(),
    "act_a": (
        "back1 in0 in1 in2 in3 th wx abs exp ln p tr0 tr1 back2 e_gap owt "
    ).split(),
    "act_b": (
        "f0 i0 g0 o0 f1 tc0 i1 g1 o1 f2 tc1 i2 g2 o2 f3 tc2 i3 g3 o3 f4 tc3 i4 g4 o4 f5 tc4 i5 g5 o5 f6 tc5 "
        "i6 g6 o6 f7 tc6 i7 g7 o7 f8 tc7 i8 g8 o8 f9 tc8 i9 g9 o9 f10 tc9 i10 g10 o10 f11 tc10 i11 g11 o11 "
        "f12 tc11 i12 g12 o12 f13 tc12 i13 g13 o13 f14 tc13 i14 g14 o14 f15 tc14 i15 g15 o15 tc15 "
    ).split(),
    "act_c": (
        "back3 q0 q1 q2 q3 k0 k1 k2 k3 v0 shift0 p0_0 p1_0 v1 shift1 p0_1 p1_1 back4 oht relu0 relu1 relu2 "
        "relu3 relu4 relu5 relu6 relu7 relu8 relu9 relu10 relu11 relu12 relu13 relu14 relu15 emit "
    ).split(),
    "dve_a": (
        "tok ln1_s ln1_mv ln1_x silu_res conv0 conv1 conv2 conv3 xc dt sum cum qk mt0 y0 yg0 mt1 y1 yg1 out "
        "ln2_s ln2_mv ln2_x lg top top_i gap e_sum w0 w1 ow1 ow owt bo "
    ).split(),
    "dve_b": (
        "take_hi take_lo ig0 c0 h0 hh0 hm0 ig1 c1 h1 hh1 hm1 ig2 c2 h2 hh2 hm2 ig3 c3 h3 hh3 hm3 ig4 c4 h4 "
        "hh4 hm4 ig5 c5 h5 hh5 hm5 ig6 c6 h6 hh6 hm6 ig7 c7 h7 hh7 hm7 ig8 c8 zz0 sum0 h2_0 h8 hh8 hm8 ig9 c9 "
        "h9 hh9 hm9 ig10 c10 h10 hh10 hm10 ig11 c11 h11 hh11 hm11 ig12 c12 h12 hh12 hm12 ig13 c13 h13 hh13 "
        "hm13 ig14 c14 h14 hh14 hm14 ig15 c15 h15 hh15 hm15 zz1 sum1 h2_1 "
    ).split(),
    "dve_c": (
        "take ln3_s ln3_mv ln3_x q0 q1 q2 q3 k0 k1 k2 k3 v0 s0_0 s1_0 own_0 den0 inv0 on0 v1 s0_1 s1_1 own_1 "
        "den1 inv1 on1 proj ln4_s ln4_mv ln4_x lg top top_i top_f oh oht moe "
    ).split(),
    "pool_a": (
        "ve1 rstd1 ve2 rstd2 "
    ).split(),
    "pool_b": (
        "mx0 mx1 mx2 hl0 mx3 hl1 mx4 hl2 mx5 hl3 mx6 hl4 mx7 hl5 mx8 hl6 mx9 hl7 mx10 hl8 mx11 hl9 mx12 hl10 "
        "mx13 hl11 mx14 hl12 mx15 hl13 hl14 hl15 "
    ).split(),
    "pool_c": (
        "ve3 rstd3 qt0 kt0 qt1 kt1 ve4 rstd4 "
    ).split(),
}



class Steps:

    def __init__(self, sem, names):
        self.sem, self.names, self.pos = sem, names, 0

    def done(self, instruction, name):
        assert self.names[self.pos] == name, (self.names[self.pos], name)
        self.pos = (self.pos + 1) % len(self.names)
        return instruction.then_inc(self.sem, 1)

    def at(self, q, name):
        return q * len(self.names) + (len(self.names) + self.names.index(name) + 1)


FIELDS = {
    "tok_w": KC * D, "in_w": 4 * D, "x_w": 2 * 80, "out_w": 2 * D, "lstm_out_w": E * D,
    "q_w": 4 * D, "k_w": 4 * D, "v_w": D, "proj_w": 2 * D, "router_w": E, "gate_w": E,
    "in_b": 4, "conv_w": 8, "conv_b": 2, "skip_d": 2,
    "out_b": 1, "lstm_b": 4 * E, "w1_b": 2 * E, "x_b": 1, "a_log": 1, "router_b": E, "gate_b": E,
    "bo": D, "b2": D,
    "ident": 128, "causal": T, "own_cols": 16, "own_row": 4, "tail_sel": 18, "iota": E, "q_lo": 1, "k_lo": 1,
    "minus_half": 3,
}
ONCE = {"tok_b": 1, "cls_a": 1, "cls_b": 1, "pos": T - 1, "band_main": 18, "band_tail": 18, "tail_heads": 2 * 128}


def field_at(fields, name):
    return sum(n for f, n in list(fields.items())[:list(fields).index(name)])


def schedule():
    a = [("tok",), ("ln", 1), ("ln_x", 1), ("ln_back", 1)] + [("in", k) for k in range(4)] + [("conv", j) for j in range(4)]
    a += [("silu",), ("xc",), ("wx",), ("softplus",), ("scan",), ("exps",), ("cb",)]
    for b in range(2):
        a += [("tr", b), ("mt", b), ("y", b)]
    a += [("out",), ("ln", 2), ("ln_x", 2), ("ln_back", 2), ("route",), ("weights",), ("owt",), ("bo",), ("scratch",)]
    c = [("take",), ("ln", 3), ("ln_x", 3), ("ln_back", 3)] + [("qk", w, p) for w in "qk" for p in range(4)]
    for b in range(2):
        c += [("v", b)] + [("smax", b, m) for m in range(2)] + [("shift", b)]
        c += [("prob", b, m) for m in range(2)] + [("pv", b)]
    c += [("proj",), ("ln", 4), ("ln_x", 4), ("ln_back", 4), ("gate",), ("oht",)]
    for n in range(2 * E):
        c += [("up", n)] + ([("down", n - 1)] if n else [])
    c += [("down", 2 * E - 1), ("emit",)]

    def placed(chain, stages, slots):
        total, so_far, found = sum(REST[s[0]] for s in stages), 0, []
        for s in stages:
            slot = int(so_far * slots / total) + NUDGE.get((chain, *s), 0)
            found.append((min(max(slot, found[-1][0] if found else 0), slots), (chain, *s)))
            so_far += REST[s[0]]
        return found

    slots = 4 * PAIR_UNITS
    b = [(0, ("B", "take")), (0, ("B", "mask_x", 0))]
    for u in range(PAIR_UNITS):
        if u + 1 < PAIR_UNITS:
            b.append((4 * u + LAG["mask_x"], ("B", "mask_x", u + 1)))
        for name in ("cell", "tanh_c", "hidden", "expert_out"):
            b.append((4 * u + LAG[name], ("B", name, u)))
        if u == E - 1:
            b.append((4 * u + LAG["expert_out"], ("B", "step_out", 0)))
        if u in (3, 7):
            b.append((4 * u + LAG["masks"], ("B", "masks", u // 4 + 2)))
    b.append((4 * (PAIR_UNITS - 1) + LAG["expert_out"], ("B", "step_out", 1)))
    waiting = placed("A", a, slots - A_LEAD) + placed("C", c, slots)
    waiting += [(slots - A_LEAD, ("A", "masks", 0)), (2 * slots, ("A", "masks", 1))]
    waiting = sorted(b[2:] + waiting, key=lambda x: x[0])
    order = [stage for _, stage in b[:2]]
    for slot in range(slots):
        order.append(("B", "gate", slot // 4, slot % 4))
        while waiting and waiting[0][0] <= slot:
            order.append(waiting.pop(0)[1])
    return order + [stage for _, stage in waiting]


def build(nc, x_t, wh, wi, wmoe, packed, once, v_ones, out, scr_onehot, scr_weight):
    NP = x_t.shape[0] - 1
    ctx = ExitStack()
    with ctx:
        def sb(name, shape, dt=F32):
            return ctx.enter_context(nc.sbuf_tensor(name, shape, dt))

        def bank(name):
            return ctx.enter_context(nc.psum_tensor(name, [128, 512], F32))

        def sem(name):
            return ctx.enter_context(nc.semaphore(name))

        packed_sb = sb("packed_sb", [128, sum(FIELDS.values())])

        def field(name, rows=128):
            at = field_at(FIELDS, name)
            return packed_sb[0:rows, at:at + FIELDS[name]]

        wh_hi, wh_lo = sb("wh_hi", [128, E * 512], R32), sb("wh_lo", [128, E * 512], R32)
        wi_hi, wi_lo = sb("wi_hi", [128, E * 512], R32), sb("wi_lo", [128, E * 512], R32)
        moe_w = sb("moe_w", [128, 4, 512])
        ident = field("ident")
        ident_r = sb("ident_r", [128, 128], R32)
        band = sb("band", [128, 3, T + 1], R32)
        tail_heads = sb("tail_heads", [8, 2, 128], R32)
        neg_a = sb("neg_a", [16, 1])
        scrap = sb("scrap", [128, 9])
        h_add = sb("h_add", [128, T])

        x_raw = sb("x_raw", [128, KC, PT])
        h_a = sb("h_a", [128, PAD])
        xn_a = sb("xn_a", [128, PAD])
        xt_a = sb("xt_a", [128, 3, 128])
        conv_in = sb("conv_in", [128, 2, 2, T + 3])
        xc = sb("xc", [128, 2, PT])
        th = sb("th", [128, 2, PT])
        gate = sb("gate", [128, 2, PT])
        ow_t = sb("ow_t", [26, PT])
        b16, c16 = ow_t[0:16, :], sb("c16", [16, PT])
        dt16, e16, s16 = xt_a[:, :, :].rearrange("p c d -> p (c d)")[0:16, 0:PT], th[0:16, 0, :], th[0:16, 1, :]

        def once_field(name, rows=128):
            at = field_at(ONCE, name)
            return gate[:, :, :].rearrange("p k t -> p (k t)")[0:rows, at:at + ONCE[name]]

        xc_t = sb("xc_t", [128, 512])
        mt = sb("mt", [128, T + TAIL])
        stats, mv = sb("stats", [128, 3, 6]), sb("mv", [128, 3, 2])
        ve, rstd = sb("ve", [128, 3]), sb("rstd", [128, 3])
        lg, top = sb("lg", [128, 3, 8]), sb("top", [128, 3, 8])
        top_i, top_f = sb("top_i", [128, 3, 8], U32), sb("top_f", [128, 3, 2])
        e_gap, e_sum = sb("e_gap", [128, 3]), sb("e_sum", [128, 3])
        ow = sb("ow", [128, 3, 26])
        ow_w = sb("ow_w", [128, 3, 8])
        ow_b = sb("ow_b", [24, PT], BF16)

        h1, h2 = sb("h1", [128, PT]), sb("h2", [128, PT])
        xb_hi, xb_lo = sb("xb_hi", [128, PT], R32), sb("xb_lo", [128, PT], R32)
        onehot = [sb(f"onehot{i}", [128, 4, 2, T], BF16) for i in range(2)]
        slot_w = [sb(f"slot_w{i}", [128, 2, T]) for i in range(2)]
        mx_hi, mx_lo = sb("mx_hi", [128, 2, PT], R32), sb("mx_lo", [128, 2, PT], R32)
        hh, hl = sb("hh", [128, E, PT], R32), sb("hl", [128, E, PT], R32)
        cell2 = sb("cell2", [128, E, PT])
        act4 = sb("act4", [128, 4, PT])
        hid2 = sb("hid2", [128, PT])
        hm = sb("hm", [128, PT])
        z_tmp = hm[:, :].rearrange("p (k t) -> p k t", k=2)

        h_c = sb("h_c", [128, PAD])
        xn_c = sb("xn_c", [128, PAD])
        xt_c = sb("xt_c", [128, 3, 128])
        stats_c, mv_c = sb("stats_c", [128, 3, 6]), sb("mv_c", [128, 3, 2])
        ve_c, rstd_c = sb("ve_c", [128, 3]), sb("rstd_c", [128, 3])
        qs, ks = sb("qs", [128, 4, PT + 2], R32), sb("ks", [128, 4, PT + 2], R32)
        q_tail, k_tail = sb("q_tail", [128, 4, 128], R32), sb("k_tail", [128, 4, 128], R32)
        v_main, v_tail = sb("v_main", [128, NH, 2 * HD]), sb("v_tail", [128, 2, 128])
        row_max, tail_max = sb("row_max", [128, 8]), sb("tail_max", [128, 2])
        tail_max_own = sb("tail_max_own", [128, 2, 4])
        shift_t = sb("shift_t", [8, T + 1], R32)
        prob = sb("prob", [128, NH * (T + 1)])
        prob_tail = sb("prob_tail", [128, 2, T])
        norm = sb("norm", [128, 2, PT])
        o_n = sb("o_n", [128, 2, PT])
        lg_c, top_c = sb("lg_c", [128, 3, 8]), sb("top_c", [128, 3, 8])
        top_ic, top_fc = sb("top_ic", [128, 3, 8], U32), sb("top_fc", [128, 3, 1])
        oh_c, oh_b = sb("oh_c", [128, 3, 8]), sb("oh_b", [8, PT], BF16)
        oh_t = xt_c[:, :, :].rearrange("p c d -> p (c d)")[0:8, 0:PT]
        out_sb = sb("out_sb", [128, 3, 128])
        relu2 = norm
        far = sb("far", [8, E], BF16)

        gates = [bank(f"gate_{g}") for g in GATES]
        z_bank, m_bank, a_bank, c_bank = bank("z_bank"), bank("m_bank"), bank("a_bank"), bank("c_bank")

        steps = {}
        for eng, chains in (("pe", "abc"), ("act", "abc"), ("dve", "abc"), ("pool", "abc")):
            for ch in chains:
                key = f"{eng}_{ch}"
                steps[key] = Steps(sem(f"{key}_done"), STEP_NAMES[key])
        pe_a, pe_b, pe_c = steps["pe_a"], steps["pe_b"], steps["pe_c"]
        act_a, act_b, act_c = steps["act_a"], steps["act_b"], steps["act_c"]
        dve_a, dve_b, dve_c = steps["dve_a"], steps["dve_b"], steps["dve_c"]
        pool_a, pool_b, pool_c = steps["pool_a"], steps["pool_b"], steps["pool_c"]
        consts_in, once_in, ones_in, x_in = sem("consts_in"), sem("once_in"), sem("ones_in"), sem("x_in")
        stage_in = [sem(f"stage_in{i}") for i in range(2)]
        split_done, setup_split, setup_misc = sem("split_done"), sem("setup_split"), sem("setup_misc")
        waited, band_zero = sem("waited"), sem("band_zero")
        moe_in = [sem(f"moe_in{i}") for i in range(4)]
        scratch_out, onehot_in = sem("scratch_out"), [sem(f"onehot_in{i}") for i in range(2)]
        slot_w_in = [sem(f"slot_w_in{i}") for i in range(2)]
        out_stored = sem("out_stored")

        order = schedule()

        def run(eng, stages, setup=()):
            def iteration(it, chains, between=()):
                between = list(between)
                for chain, name, *args in order:
                    part = stages.get((chain, name))
                    if chain in chains and part:
                        part(it + {"A": 1, "B": 0, "C": -1}[chain], *args)
                        if between:
                            between.pop(0)()
                assert not between

            iteration(-1, "A", setup)
            iteration(0, "AB")
            with eng.Fori(1, NP - 1) as it:
                iteration(it, "ABC")
            iteration(NP - 1, "BC")
            iteration(NP, "C")

        def first(q):
            return isinstance(q, int) and q == 0

        def after(eng, who, q, name):
            eng.wait_ge(who.sem, who.at(q, name))

        def before(eng, who, q, name):
            eng.wait_ge(who.sem, who.at(q, name) - len(who.names))

        def plain(eng):
            eng.sem_inc(waited, 1)

        def two(ap):
            return ap.rearrange("p (b t) -> p b t", b=2)

        def rows(head):
            side = head % 2
            return slice(64 * side, 64 * side + 64)

        def spread(ap, axis, n):
            ap = ap.unsqueeze(axis)
            shape = list(ap.shape)
            shape[axis] = n
            return ap.broadcast_to(shape)

        def heads_of(m, side):
            return range(side, 6, 2) if m == 0 else range(6 + side, 7 + side)

        def turn(w, p):
            return p if w == "q" else 4 + p

        def qk_bank(n):
            return (c_bank, m_bank)[n % 2]

        def qk_hi(n):
            return norm[:, n % 2, :].bitcast(R32)

        def per_head(bank_, n):
            return bank_[:, 0:n * (T + 1)].rearrange("p (h t) -> p h t", t=T + 1)[:, :, 0:T]

        def dram_rows(ap, rows_, dims, offset=0):
            return bass.AP(ap.tensor, offset, [[0, rows_]] + dims)

        block = ctx.enter_context(nc.Block())

        @block.sync
        def _(sp):
            sp.dma_start(packed_sb[:, :], packed).then_inc(consts_in, 16)
            sp.dma_start(gate[:, :, :].rearrange("p k t -> p (k t)")[:, 0:sum(ONCE.values())], once
                         ).then_inc(once_in, 16)
            stage = cell2[:, :, :].rearrange("p e t -> p (e t)")
            sp.dma_start(x_raw[:, :, :], x_t[0]).then_inc(x_in, 16)
            for c in range(8):
                src = (wh if c < 4 else wi)[:, (c % 4) * 1024:(c % 4 + 1) * 1024]
                if c >= 2:
                    sp.wait_ge(split_done, c - 1)
                sp.dma_start(stage[:, (c % 2) * 1024:(c % 2 + 1) * 1024], src).then_inc(stage_in[c % 2], 16)
                if c == 1:
                    sp.dma_start(v_main[:, :, :].rearrange("p h c -> p (h c)"), v_ones[:, 0:256]).then_inc(ones_in, 16)
                    sp.dma_start(v_tail[:, :, :].rearrange("p g c -> p (g c)"), v_ones[:, 256:512]).then_inc(ones_in, 16)
            for e in range(4):
                sp.dma_start(moe_w[:, e, :], wmoe[e]).then_inc(moe_in[e], 16)

            def load_x(q):
                after(sp, pe_a, q, "tok")
                sp.dma_start(x_raw[:, :, :], x_t[q + 1]).then_inc(x_in, 16)

            def scratch(q):
                after(sp, act_a, q, "owt")
                after(sp, dve_a, q, "owt")
                plain(sp)
                if not first(q):
                    for i in range(2):
                        sp.wait_ge(onehot_in[i], 32 * q)
                        sp.wait_ge(slot_w_in[i], 16 * q)
                for k in range(2):
                    sp.dma_start(scr_onehot[:, :, k, :].rearrange("b e t -> e b t"),
                                 two(ow_b[8 + 8 * k:16 + 8 * k, :])).then_inc(scratch_out, 16)
                sp.dma_start(scr_weight.rearrange("b k t -> k b t"), two(ow_t[24:26, :])).then_inc(scratch_out, 16)

            def load_onehot(q, hs):
                b, half = hs // 2, hs % 2
                sp.dma_start(onehot[half][:, :, :, :].rearrange("p e k t -> p (e k t)"),
                             dram_rows(scr_onehot, 128, [[1, 8 * T]], (b * E + 4 * half) * 2 * T)
                             ).then_inc(onehot_in[half], 16)

            def masks_a(q, b):
                if b == 0:
                    sp.wait_ge(scratch_out, q * 48 + 48)
                    plain(sp)
                if not first(q):
                    after(sp, dve_b, q - 1, f"hm{11 + 4 * b}")
                load_onehot(q, b)
                if not first(q):
                    after(sp, dve_b, q - 1, f"zz{b}")
                sp.dma_start(slot_w[b][:, :, :].rearrange("p k t -> p (k t)"),
                             dram_rows(scr_weight, 128, [[1, PT]], b * PT)).then_inc(slot_w_in[b], 16)

            def masks_b(q, hs):
                after(sp, dve_b, q, f"hm{4 * hs - 5}")
                load_onehot(q, hs)

            def moe_next(q, n):
                if n % 2:
                    e = n // 2
                    after(sp, pe_c, q, f"down{n}")
                    sp.dma_start(moe_w[:, e % 4, :], wmoe[(e + 4) % E]).then_inc(moe_in[e % 4], 16)

            def emit(q):
                after(sp, act_c, q, "emit")
                base = q * PT
                sp.dma_start(out[bass.ds(base, 256), :].rearrange("(c p) d -> p c d", c=2), out_sb[:, 0:2, :]
                             ).then_inc(out_stored, 16)
                sp.dma_start(out[bass.ds(base + 256, PT - 256), :], out_sb[0:PT - 256, 2, :]).then_inc(out_stored, 16)
                sp.wait_ge(out_stored, q * 32 + 32)
                plain(sp)

            run(sp, {("A", "tok"): load_x, ("A", "scratch"): scratch, ("A", "masks"): masks_a,
                     ("B", "masks"): masks_b, ("C", "down"): moe_next, ("C", "emit"): emit})
            sp.wait_ge(out_stored, 32 * NP)
            sp.wait_ge(scratch_out, 48 * NP)
            sp.wait_ge(x_in, 16 * (NP + 1))
            for i in range(4):
                sp.wait_ge(moe_in[i], 16 * (2 * NP + 1))

        @block.tensor
        def _(pe):
            pe.wait_ge(consts_in, 16)
            pe.wait_ge(setup_misc, 1)
            for who, where in ((pe_a, a_bank), (pe_c, c_bank), (pe_b, z_bank)):
                pe.matmul(where[:, 0:128], ident, ident, start=True, stop=True).then_inc(who.sem, len(who.names))

            def transposes(src, dst, where):
                for c in range(3):
                    last = pe.transpose(where[:, c * 128:(c + 1) * 128], src[c], ident)
                return last

            def chunks(tile):
                return [tile[:, c * 128:(c + 1) * 128] for c in range(3)]

            def tok(q):
                pe.wait_ge(x_in, q * 16 + 16)
                before(pe, dve_a, q, "bo")
                for c in range(KC):
                    last = pe.matmul(a_bank[:, 0:PT], field("tok_w")[:, c * D:(c + 1) * D], x_raw[:, c, :],
                                     start=c == 0, stop=c == KC - 1)
                pe_a.done(last, "tok")

            def ln(who, dve, src, where, ready):
                def part(q, n):
                    after(pe, dve, q, ready[n])
                    if n == 3:
                        before(pe, act_c, q, "emit")
                    who.done(transposes(chunks(src), None, where), f"ln{n}")
                return part

            def ln_back(who, dve, xt, where):
                def part(q, n):
                    after(pe, dve, q, f"ln{n}_x")
                    who.done(transposes([xt[:, c, :] for c in range(3)], None, where), f"back{n}")
                return part

            def in_proj(q, k):
                after(pe, act_a, q, f"in{k - 1}" if k else "back1")
                pe_a.done(pe.matmul(a_bank[:, 0:PT], field("in_w")[:, k * D:(k + 1) * D], xn_a[:, 0:PT],
                                    start=True, stop=True), f"in{k}")

            def wx(q):
                after(pe, act_a, q, "in3")
                after(pe, dve_a, q, "xc")
                for k in range(2):
                    last = pe.matmul(a_bank[0:80, 0:PT], field("x_w")[:, k * 80:(k + 1) * 80], xc[:, k, :],
                                     start=k == 0, stop=k == 1)
                pe_a.done(last, "wx")

            def tr(q, b):
                if b == 0:
                    after(pe, act_a, q, "wx")
                else:
                    after(pe, dve_a, q, "yg0")
                for k in range(2):
                    pe.transpose(a_bank[:, k * 128:(k + 1) * 128], xc[:, k, b * T:b * T + 128], ident)
                    last = pe.transpose(a_bank[0:TAIL, 256 + k * 128:384 + k * 128],
                                        xc[:, k, b * T + 128:b * T + T], ident)
                pe_a.done(last, f"tr{b}")

            def mt_part(q, b):
                after(pe, act_a, q, f"tr{b}")
                after(pe, dve_a, q, "qk")
                pe.matmul(a_bank[:, 0:T], b16[:, b * T:b * T + 128], c16[:, b * T:b * T + T], start=True, stop=True)
                pe_a.done(pe.matmul(a_bank[0:TAIL, T:T + TAIL], b16[:, b * T + 128:b * T + T],
                                    c16[:, b * T + 128:b * T + T], start=True, stop=True), f"mt{b}")

            def y(q, b):
                after(pe, dve_a, q, f"mt{b}")
                for k in range(2):
                    pe.matmul(a_bank[:, k * T:k * T + T], xc_t[:, k * 128:(k + 1) * 128], mt[:, 0:T],
                              start=True, stop=False)
                    last = pe.matmul(a_bank[:, k * T + 128:k * T + T], xc_t[0:TAIL, 256 + k * 128:384 + k * 128],
                                     mt[0:TAIL, T:T + TAIL], start=False, stop=True)
                pe_a.done(last, f"y{b}")

            def out_proj(q):
                after(pe, dve_a, q, "yg1")
                for k in range(2):
                    last = pe.matmul(a_bank[:, 0:PT], field("out_w")[:, k * D:(k + 1) * D], gate[:, k, :],
                                     start=k == 0, stop=k == 1)
                pe_a.done(last, "out")

            def logits(who, act, xn, w, where, name, evac):
                def part(q):
                    after(pe, act, q, evac)
                    for c in range(3):
                        last = pe.matmul(where[:, c * 8:c * 8 + 8], xn[:, c * 128:(c + 1) * 128], field(w),
                                         start=True, stop=True)
                    who.done(last, name)
                return part

            def owt(q):
                after(pe, dve_a, q, "ow")
                for c in range(3):
                    last = pe.matmul(a_bank[0:26, c * 128:(c + 1) * 128], ow[:, c, :], ident, start=True, stop=True)
                pe_a.done(last, "owt")

            def bo(q):
                after(pe, act_a, q, "owt")
                after(pe, dve_a, q, "owt")
                pe_a.done(pe.matmul(a_bank[:, 0:PT], field("bo", 8), ow_t[0:8, :], start=True, stop=True), "bo")

            def gate_part(q, u, g):
                e = u % E
                if u:
                    after(pe, act_b, q, f"{GATES[g]}{u - 1}")
                else:
                    before(pe, act_b, q, f"{GATES[g]}{PAIR_UNITS - 1}")
                if g == 0:
                    after(pe, pool_b, q, f"mx{u}")
                    if u < E:
                        before(pe, pool_b, q, f"hl{u + E}")
                    else:
                        after(pe, pool_b, q, f"hl{u - E}")
                w = slice(e * 512 + g * 128, e * 512 + (g + 1) * 128)
                parts = ((wi_hi, mx_hi[:, u % 2, :]), (wi_lo, mx_hi[:, u % 2, :]), (wi_hi, mx_lo[:, u % 2, :]),
                         (wh_hi, hh[:, e, :]), (wh_lo, hh[:, e, :]), (wh_hi, hl[:, e, :]))
                for n, (weight, moving) in enumerate(parts):
                    last = pe.matmul(gates[g][:, 0:PT], weight[:, w], moving, start=n == 0, stop=n == 5)
                pe_b.done(last, f"{GATES[g]}{u}")

            def expert_out(q, u):
                e = u % E
                after(pe, dve_b, q, f"hm{u}")
                if e == 0:
                    if u:
                        after(pe, dve_b, q, "zz0")
                    else:
                        before(pe, dve_b, q, "zz1")
                pe_b.done(pe.matmul(z_bank[:, 0:PT], field("lstm_out_w")[:, e * D:(e + 1) * D], hm[:, :],
                                    start=e == 0, stop=e == E - 1), f"z{u}")

            def qk(q, w, p):
                n = turn(w, p)
                if n == 0:
                    after(pe, act_c, q, "back3")
                elif n == 1:
                    before(pe, dve_c, q, "moe")
                else:
                    after(pe, dve_c, q, f"q{n - 2}" if n < 6 else f"k{n - 6}")
                pe_c.done(pe.matmul(qk_bank(n)[:, 0:PT], field(f"{w}_w")[:, p * 128:(p + 1) * 128], xn_c[:, 0:PT],
                                    start=True, stop=True), f"{w}{p}")

            def v(q, b):
                if b:
                    after(pe, act_c, q, "p1_0")
                else:
                    after(pe, dve_c, q, "k2")
                pe.matmul(c_bank[:, 0:128], xn_c[:, b * T:b * T + 128], field("v_w"), start=True, stop=True)
                for j in range(4):
                    last = pe.matmul(c_bank[32 * j:32 * j + 32, 128:256], xn_c[:, b * T + 128:b * T + 160],
                                     field("v_w"), start=True, stop=True)
                pe_c.done(last, f"v{b}")

            def bands(m):
                n = len(heads_of(m, 0))
                pe.matmul(m_bank[:, 0:n * (T + 1)], ident_r[:, :], spread(band[:, 0, :], 1, n), start=True, stop=False)
                moving = band[:, :, :] if m else spread(band[:, 0, :], 1, n)
                pe.matmul(c_bank[:, 0:3 * (T + 1)], ident_r[:, :], moving, start=True, stop=False)

            def ends(m, n, side):
                return n == len(heads_of(m, 0)) - 1 and not (m and side == 0)

            def smax(q, b, m):
                if m == 0:
                    after(pe, act_c, q, f"v{b}")
                    after(pe, dve_c, q, f"v{b}")
                else:
                    after(pe, dve_c, q, f"s0_{b}")
                    after(pe, pool_c, q, f"kt{b}")
                cols = slice(b * T, b * T + T + 1)
                bands(m)
                for n in range(len(heads_of(m, 0))):
                    at = n * (T + 1)
                    for side, where in enumerate((c_bank, m_bank)):
                        h = heads_of(m, side)[n]
                        last = pe.matmul(where[:, at:at + T + 1], qs[rows(h), h // 2, b * T:b * T + 128],
                                         ks[rows(h), h // 2, cols], start=False, stop=ends(m, n, side))
                for g in range(2 * m):
                    at = (1 + g) * (T + 1)
                    for r in range(2):
                        last = pe.matmul(c_bank[:, at:at + T + 1], q_tail[:, 2 * g + r, :], ks[:, 2 * g + r, cols],
                                         start=False, stop=(g, r) == (1, 1))
                pe_c.done(last, f"s{m}_{b}")

            def shift(q, b):
                after(pe, dve_c, q, f"own_{b}")
                pe.matmul(c_bank[0:8, 0:128], row_max[:, :], ident, start=True, stop=True)
                pe_c.done(pe.matmul(c_bank[0:8, 128:146], tail_max_own[:, :, :].rearrange("p g j -> p (g j)"),
                                    field("tail_sel"), start=True, stop=True), f"shift{b}")

            def prob_part(q, b, m):
                after(pe, act_c, q, f"p0_{b}" if m else f"shift{b}")
                cols = slice(b * T, b * T + T + 1)
                bands(m)
                for n in range(len(heads_of(m, 0))):
                    at = n * (T + 1)
                    for side, where in enumerate((c_bank, m_bank)):
                        h = heads_of(m, side)[n]
                        pe.matmul(where[:, at:at + T + 1], ks[rows(h), h // 2, b * T:b * T + 128],
                                  qs[rows(h), h // 2, cols], start=False, stop=False)
                    for side, where in enumerate((c_bank, m_bank)):
                        h = heads_of(m, side)[n]
                        last = pe.matmul(where[:, at:at + T + 1], ident_r[0:8, h:h + 1].broadcast_to([8, 128]),
                                         shift_t[:, :], start=False, stop=ends(m, n, side))
                for g in range(2 * m):
                    at = (1 + g) * (T + 1)
                    for r in range(2):
                        pe.matmul(c_bank[:, at:at + T + 1], k_tail[:, 2 * g + r, :], qs[:, 2 * g + r, cols],
                                  start=False, stop=False)
                    last = pe.matmul(c_bank[:, at:at + T + 1], tail_heads[:, g, :], shift_t[:, :], start=False, stop=g == 1)
                pe_c.done(last, f"p{m}_{b}")

            def pv(q, b):
                after(pe, act_c, q, f"p1_{b}")
                for g in range(2):
                    at = g * (T + 1)
                    for j in range(4):
                        h = 4 * g + j
                        pe.matmul(m_bank[32 * j:32 * j + 32, at:at + T], v_main[:, h, :],
                                  prob[:, h * (T + 1):h * (T + 1) + T], start=True, stop=False)
                    last = pe.matmul(m_bank[:, at:at + T], v_tail[:, g, :], prob_tail[:, g, :], start=False, stop=True)
                pe_c.done(last, f"pv{b}")

            def proj(q):
                after(pe, dve_c, q, "on1")
                for g in range(2):
                    last = pe.matmul(c_bank[:, 0:PT], field("proj_w")[:, g * D:(g + 1) * D], o_n[:, g, :],
                                     start=g == 0, stop=g == 1)
                pe_c.done(last, "proj")

            def oht(q):
                after(pe, dve_c, q, "oh")
                for c in range(3):
                    last = pe.matmul(c_bank[0:8, c * 128:(c + 1) * 128], oh_c[:, c, :], ident, start=True, stop=True)
                pe_c.done(last, "oht")

            def up(q, n):
                e, k = n // 2, n % 2
                if n == 0:
                    after(pe, dve_c, q, "oht")
                    after(pe, act_c, q, "back4")
                else:
                    after(pe, act_c, q, f"relu{n - 1}")
                pe.wait_ge(moe_in[e % 4], q * 32 + 16 * (e // 4) + 16)
                pe.matmul(c_bank[:, 0:PT], moe_w[:, e % 4, k * 128:(k + 1) * 128], xn_c[:, 0:PT], start=True, stop=False)
                pe_c.done(pe.matmul(c_bank[:, 0:PT], far[:, e:e + 1].broadcast_to([8, 128]), oh_b[:, :],
                                    start=False, stop=True), f"up{n}")

            def down(q, n):
                e, k = n // 2, n % 2
                if n == 0:
                    after(pe, act_c, q, "oht")
                    pe.matmul(m_bank[:, 0:PT], field("b2", 8), oh_t[:, :], start=True, stop=False)
                after(pe, act_c, q, f"relu{n}")
                pe_c.done(pe.matmul(m_bank[:, 0:PT], moe_w[:, e % 4, 256 + k * 128:384 + k * 128], relu2[:, n % 2, :],
                                    start=False, stop=n == 2 * E - 1), f"down{n}")

            def emit(q):
                after(pe, act_c, q, f"relu{2 * E - 1}")
                after(pe, dve_c, q, "moe")
                pe_c.done(transposes(chunks(h_c), None, c_bank), "emit")

            ln_a = ln(pe_a, dve_a, h_a, a_bank, {1: "tok", 2: "out"})
            ln_c = ln(pe_c, dve_c, h_c, c_bank, {3: "take", 4: "proj"})
            run(pe, {("A", "tok"): tok, ("A", "ln"): ln_a, ("A", "ln_back"): ln_back(pe_a, dve_a, xt_a, a_bank),
                     ("A", "in"): in_proj, ("A", "wx"): wx, ("A", "tr"): tr, ("A", "mt"): mt_part, ("A", "y"): y,
                     ("A", "out"): out_proj,
                     ("A", "route"): logits(pe_a, act_a, xn_a, "router_w", a_bank, "logits", "back2"),
                     ("A", "owt"): owt, ("A", "bo"): bo,
                     ("B", "gate"): gate_part, ("B", "expert_out"): expert_out,
                     ("C", "ln"): ln_c, ("C", "ln_back"): ln_back(pe_c, dve_c, xt_c, c_bank),
                     ("C", "qk"): qk, ("C", "v"): v, ("C", "smax"): smax, ("C", "shift"): shift,
                     ("C", "prob"): prob_part, ("C", "pv"): pv, ("C", "proj"): proj,
                     ("C", "gate"): logits(pe_c, act_c, xn_c, "gate_w", c_bank, "logits", "back4"),
                     ("C", "oht"): oht, ("C", "up"): up, ("C", "down"): down, ("C", "emit"): emit})

        @block.scalar
        def _(act):
            act.wait_ge(consts_in, 16)
            act.activation(neg_a[:, :], field("a_log", 16), ACT.Exp).then_inc(setup_misc, 1)
            act.wait_ge(setup_misc, 2)
            for n, who in enumerate((act_a, act_b, act_c)):
                act.activation(scrap[:, n:n + 1], field("minus_half")[:, 0:1], ACT.Copy).then_inc(who.sem, len(who.names))

            def back(who, pe_, xn, where):
                def part(q, n):
                    after(act, pe_, q, f"back{n}")
                    if who is act_a and not first(q):
                        before(act, dve_b, q, "take_lo")
                    who.done(act.activation(xn[:, 0:PT], where[:, 0:PT], ACT.Copy), f"back{n}")
                return part

            def in_part(q, k):
                after(act, pe_a, q, f"in{k}")
                bias = field("in_b")[:, k:k + 1]
                if k < 2:
                    act_a.done(act.activation(conv_in[:, k, :, 3:3 + T], two(a_bank[:, 0:PT]), ACT.Identity,
                                              bias=bias), f"in{k}")
                else:
                    act.activation(gate[:, k - 2, :], a_bank[:, 0:PT], ACT.Identity, bias=bias, scale=0.5)
                    act_a.done(act.activation(th[:, k - 2, :], a_bank[:, 0:PT], ACT.Tanh, bias=bias, scale=0.5),
                               f"in{k}")

            def silu(q):
                after(act, dve_a, q, "conv3")
                after(act, dve_a, q, "silu_res")
                act_a.done(act.activation(th[:, :, :], xc[:, :, :], ACT.Tanh), "th")

            def wx(q):
                after(act, pe_a, q, "wx")
                if not first(q):
                    act.wait_ge(scratch_out, q * 48)
                bias = field("x_b")
                act.activation(b16[:, :], a_bank[0:16, 0:PT], ACT.Identity, bias=bias[0:16])
                act.activation(c16[:, :], a_bank[32:48, 0:PT], ACT.Identity, bias=bias[32:48])
                act_a.done(act.activation(dt16[:, :], a_bank[64:80, 0:PT], ACT.Identity, bias=bias[64:80]), "wx")

            def softplus(q):
                after(act, act_a, q, "wx")
                act_a.done(act.activation(e16[:, :], dt16[:, :], ACT.Abs), "abs")
                after(act, act_a, q, "abs")
                act_a.done(act.activation(e16[:, :], e16[:, :], ACT.Exp, scale=-1.0), "exp")
                after(act, act_a, q, "exp")
                act_a.done(act.activation(e16[:, :], e16[:, :], ACT.Ln, bias=1.0), "ln")

            def exps(q):
                after(act, dve_a, q, "cum")
                act.activation(e16[:, :], dt16[:, :], ACT.Exp)
                act_a.done(act.activation(s16[:, :], dt16[:, :], ACT.Exp, scale=-1.0), "p")

            def tr(q, b):
                after(act, pe_a, q, f"tr{b}")
                act.activation(xc_t[:, 0:256], a_bank[:, 0:256], ACT.Copy)
                act_a.done(act.activation(xc_t[0:TAIL, 256:512], a_bank[0:TAIL, 256:512], ACT.Copy), f"tr{b}")

            def weights(q):
                after(act, dve_a, q, "gap")
                act_a.done(act.activation(e_gap[:, :], e_gap[:, :], ACT.Exp), "e_gap")

            def owt(q):
                after(act, pe_a, q, "owt")
                act_a.done(act.activation(ow_t[:, :], a_bank[0:26, 0:PT], ACT.Copy), "owt")

            def gate_part(q, u, g):
                e = u % E
                after(act, pe_b, q, f"{GATES[g]}{u}")
                if g == 0:
                    if u:
                        after(act, dve_b, q, f"c{u - 1}")
                    else:
                        before(act, dve_b, q, f"c{PAIR_UNITS - 1}")
                if g == 3 and u == 0:
                    before(act, dve_b, q, f"h{PAIR_UNITS - 1}")
                if g == 3 and u:
                    after(act, dve_b, q, f"h{u - 1}")
                act_b.done(act.activation(act4[:, g, :], gates[g][:, 0:PT], ACT.Tanh,
                                          bias=field("lstm_b")[:, 4 * e + g:4 * e + g + 1],
                                          scale=1.0 if g == 2 else 0.5), f"{GATES[g]}{u}")

            def tanh_c(q, u):
                after(act, dve_b, q, f"c{u}")
                if u:
                    after(act, dve_b, q, f"hm{u - 1}")
                    after(act, pool_b, q, f"hl{u - 1}")
                else:
                    before(act, dve_b, q, f"hm{PAIR_UNITS - 1}")
                    before(act, pool_b, q, f"hl{PAIR_UNITS - 1}")
                act_b.done(act.activation(hid2[:, :], cell2[:, u % E, :], ACT.Tanh, scale=0.5), f"tc{u}")

            def qk(q, w, p):
                after(act, pe_c, q, f"{w}{p}")
                n = turn(w, p)
                act_c.done(act.activation(qk_hi(n), qk_bank(n)[:, 0:PT], ACT.Copy), f"{w}{p}")

            def v(q, b):
                after(act, pe_c, q, f"v{b}")
                act_c.done(act.activation(v_main[:, :, 0:HD], c_bank[:, 0:128].rearrange("p (h d) -> p h d", h=NH), ACT.Copy),
                           f"v{b}")

            def shift(q, b):
                after(act, pe_c, q, f"shift{b}")
                act_c.done(act.activation(shift_t[:, :], c_bank[0:8, 0:T + 1], ACT.Copy, scale=-1.0), f"shift{b}")

            def prob_part(q, b, m):
                after(act, pe_c, q, f"p{m}_{b}")
                scale = float(D) ** -0.5
                for side, where in enumerate((c_bank, m_bank)):
                    hs = heads_of(m, side)
                    dst = prob[:, :].rearrange("p (h t) -> p h t", t=T + 1)[:, hs[0]:hs[-1] + 1:2, 0:T]
                    ins = act.activation(dst, per_head(where, len(hs)), ACT.Exp, scale=scale)
                if m:
                    ins = act.activation(prob_tail[:, :, :], per_head(c_bank, 3)[:, 1:3], ACT.Exp, scale=scale)
                act_c.done(ins, f"p{m}_{b}")

            def oht(q):
                after(act, pe_c, q, "oht")
                act_c.done(act.activation(oh_t[:, :], c_bank[0:8, 0:PT], ACT.Copy), "oht")

            def up(q, n):
                after(act, pe_c, q, f"up{n}")
                act_c.done(act.activation(relu2[:, n % 2, :], c_bank[:, 0:PT], ACT.Relu,
                                          bias=field("w1_b")[:, n:n + 1]), f"relu{n}")

            def emit(q):
                after(act, pe_c, q, "emit")
                act_c.done(act.activation(out_sb[:, :, :].rearrange("p c d -> p (c d)"), c_bank[:, 0:PAD], ACT.Copy), "emit")

            run(act, {("A", "ln_back"): back(act_a, pe_a, xn_a, a_bank), ("A", "in"): in_part, ("A", "silu"): silu,
                      ("A", "wx"): wx, ("A", "softplus"): softplus, ("A", "exps"): exps, ("A", "tr"): tr,
                      ("A", "weights"): weights, ("A", "owt"): owt,
                      ("B", "gate"): gate_part, ("B", "tanh_c"): tanh_c,
                      ("C", "ln_back"): back(act_c, pe_c, xn_c, c_bank), ("C", "qk"): qk, ("C", "v"): v,
                      ("C", "shift"): shift, ("C", "prob"): prob_part, ("C", "oht"): oht, ("C", "up"): up,
                      ("C", "emit"): emit})

        @block.gpsimd
        def _(pool):
            pool.wait_ge(consts_in, 16)
            pool.wait_ge(setup_misc, 2)
            for n, who in enumerate((pool_a, pool_b, pool_c)):
                pool.memset(scrap[:, 3 + n:4 + n], 0.0).then_inc(who.sem, len(who.names))

            def ln(who, dve, mv_, ve_, rstd_):
                def part(q, n):
                    after(pool, dve, q, f"ln{n}_mv")
                    plain(pool)
                    who.done(pool.tensor_scalar(ve_[:, :], mv_[:, :, 1], LN_EPS, None, ALU.add), f"ve{n}")
                    after(pool, who, q, f"ve{n}")
                    who.done(pool.tensor_tensor(rstd_[:, :], ve_[:, :], field("minus_half"), ALU.pow), f"rstd{n}")
                return part

            def mask_x(q, u):
                b, e = u // E, u % E
                if u >= 2:
                    after(pool, pe_b, q, f"o{u - 2}")
                else:
                    before(pool, pe_b, q, f"o{u + PAIR_UNITS - 2}")
                if u == 0:
                    after(pool, dve_b, q, "take_lo")
                hs = u // 4
                if u % 4 == 0:
                    pool.wait_ge(onehot_in[hs % 2], q * 32 + 16 * (hs // 2) + 16)
                mask = onehot[hs % 2][:, e % 4, :, :]
                pool.tensor_tensor(two(mx_hi[:, u % 2, :]), spread(xb_hi[:, b * T:b * T + T], 1, 2), mask, ALU.mult)
                pool_b.done(pool.tensor_tensor(two(mx_lo[:, u % 2, :]), spread(xb_lo[:, b * T:b * T + T], 1, 2), mask,
                                               ALU.mult), f"mx{u}")

            def hidden_lo(q, u):
                after(pool, dve_b, q, f"hh{u}")
                pool_b.done(pool.tensor_tensor(hl[:, u % E, :], hid2[:, :], hh[:, u % E, :], ALU.subtract), f"hl{u}")

            def tails(q, b):
                after(pool, dve_c, q, "k3")
                if b:
                    after(pool, pe_c, q, "p1_0")
                else:
                    before(pool, pe_c, q, "p1_1")
                own = spread(field("own_cols").rearrange("p (a j) -> p a j", a=4), 3, TAIL)
                for dst, src, name in ((q_tail, qs, "qt"), (k_tail, ks, "kt")):
                    pool_c.done(pool.tensor_tensor(
                        dst[:, :, :].rearrange("p a (j i) -> p a j i", j=4)[:, :, :, 0:TAIL],
                        spread(src[:, :, b * T + 128:b * T + T], 2, 4), own, ALU.mult), f"{name}{b}")

            run(pool, {("A", "ln"): ln(pool_a, dve_a, mv, ve, rstd), ("B", "mask_x"): mask_x, ("B", "hidden"): hidden_lo,
                       ("C", "ln"): ln(pool_c, dve_c, mv_c, ve_c, rstd_c), ("C", "v"): tails})

        @block.vector
        def _(dve):
            for tile in (h_a, xn_a, h_c, xn_c):
                dve.memset(tile[:, PT:PAD], 0.0)
            for tile in (hh, hl, q_tail, k_tail):
                dve.memset(tile[:, :, :].bitcast(F32), 0.0)
            dve.memset(band[:, :, :].bitcast(F32), 0.0).then_inc(band_zero, 1)
            for tile in (qs, ks):
                dve.memset(tile[:, :, PT:PT + 2].bitcast(F32), 0.0)
            dve.memset(conv_in[:, :, :, 0:3], 0.0)
            dve.wait_ge(consts_in, 16)
            dve.wait_ge(once_in, 16)
            dve.wait_ge(band_zero, 1)
            dve.tensor_copy(ident_r[:, :], ident)
            dve.tensor_scalar(far[:, :], ident[0:8, 0:E], 1e30, None, ALU.mult)
            dve.tensor_copy(band[:, 0, 128:T + 1], once_field("band_main"))
            dve.tensor_copy(band[:, 1:3, 0:18], spread(once_field("band_tail"), 1, 2))
            dve.tensor_copy(tail_heads[:, :, :].rearrange("p g c -> p (g c)"), once_field("tail_heads", 8))
            for name, cols in (("lstm_out_w", slice(None)), ("conv_w", slice(None)), ("conv_b", slice(None)),
                               ("in_b", slice(2, 4))):
                dve.tensor_scalar(field(name)[:, cols], field(name)[:, cols], 0.5, None, ALU.mult)
            for g in (0, 1, 3):
                bias = field("lstm_b").rearrange("p (e g) -> p g e", g=4)[:, g, :]
                dve.tensor_scalar(bias, bias, 0.5, None, ALU.mult)
            dve.tensor_copy(h_add[:, 0:1], once_field("cls_a"))
            dve.tensor_tensor(h_add[:, 1:2], once_field("cls_b"), once_field("pos")[:, 0:1], ALU.add)
            dve.tensor_scalar(h_add[:, 2:T], once_field("pos")[:, 1:T - 1], once_field("tok_b"), None, ALU.add)
            dve.wait_ge(setup_misc, 1)
            dve.tensor_scalar(neg_a[:, :], neg_a[:, :], -1.0, None, ALU.mult).then_inc(setup_misc, 1)
            dve.wait_ge(setup_misc, 2)
            for n, who in enumerate((dve_a, dve_c)):
                dve.memset(scrap[:, 6 + n:7 + n], 0.0).then_inc(who.sem, len(who.names))
            stage = cell2[:, :, :].rearrange("p e t -> p (e t)")

            def split(c):
                hi, lo = (wh_hi, wh_lo) if c < 4 else (wi_hi, wi_lo)
                cols, src = slice((c % 4) * 1024, (c % 4 + 1) * 1024), stage[:, (c % 2) * 1024:(c % 2 + 1) * 1024]
                scale = 0.5 if c < 4 else 1.0
                dve.wait_ge(stage_in[c % 2], 16 * (c // 2) + 16)
                dve.tensor_scalar(hi[:, cols], src, scale, None, ALU.mult).then_inc(setup_split, 1)
                dve.wait_ge(setup_split, c + 1)
                dve.scalar_tensor_tensor(lo[:, cols], src, scale, hi[:, cols], ALU.mult, ALU.subtract
                                         ).then_inc(split_done, 1)

            def first_cells():
                dve.wait_ge(split_done, 8)
                dve.memset(cell2[:, :, :], 0.0).then_inc(dve_b.sem, len(dve_b.names))

            def tok(q):
                after(dve, pe_a, q, "tok")
                dve_a.done(dve.tensor_tensor(two(h_a[:, 0:PT]), two(a_bank[:, 0:PT]), spread(h_add[:, :], 1, 2), ALU.add),
                           "tok")

            def ln(who, pe_, pool_, where, stats_, mv_, rstd_, xt):
                def part(q, n):
                    after(dve, pe_, q, f"ln{n}")
                    for c in range(3):
                        ins = dve.bn_stats(stats_[:, c, :], where[:, c * 128:(c + 1) * 128])
                    who.done(ins, f"ln{n}_s")
                    after(dve, who, q, f"ln{n}_s")
                    plain(dve)
                    for c in range(3):
                        ins = dve.bn_aggr(mv_[:, c, :], stats_[:, c, :])
                    who.done(ins, f"ln{n}_mv")
                return part

            def ln_x(who, pool_, where, mv_, rstd_, xt):
                def part(q, n):
                    after(dve, who, q, f"ln{n}_mv")
                    after(dve, pool_, q, f"rstd{n}")
                    for c in range(3):
                        ins = dve.tensor_scalar(xt[:, c, :], where[:, c * 128:(c + 1) * 128], mv_[:, c, 0:1],
                                                rstd_[:, c:c + 1], ALU.subtract, ALU.mult)
                    who.done(ins, f"ln{n}_x")
                return part

            def silu_res(q, k):
                if k == 3:
                    after(dve, act_a, q, "in3")
                    dve_a.done(dve.scalar_tensor_tensor(gate[:, :, :], th[:, :, :], 1.0, gate[:, :, :], ALU.add, ALU.mult),
                               "silu_res")

            def conv(q, j):
                if j:
                    after(dve, dve_a, q, f"conv{j - 1}")
                else:
                    after(dve, act_a, q, "in1")
                for k in range(2):
                    w = field("conv_w")[:, 4 * k + j:4 * k + j + 1]
                    src, dst = conv_in[:, k, :, j:j + T], two(xc[:, k, :])
                    if j == 0:
                        ins = dve.tensor_scalar(dst, src, w, field("conv_b")[:, k:k + 1], ALU.mult, ALU.add)
                    else:
                        ins = dve.scalar_tensor_tensor(dst, src, w, dst, ALU.mult, ALU.add)
                dve_a.done(ins, f"conv{j}")

            def silu_x(q):
                after(dve, act_a, q, "th")
                dve_a.done(dve.scalar_tensor_tensor(xc[:, :, :], th[:, :, :], 1.0, xc[:, :, :], ALU.add, ALU.mult), "xc")

            def scan(q):
                after(dve, act_a, q, "ln")
                dve_a.done(dve.scalar_tensor_tensor(dt16[:, :], dt16[:, :], 0.0, e16[:, :], ALU.max, ALU.add), "dt")
                after(dve, dve_a, q, "dt")
                for b in range(2):
                    cols = slice(b * T, b * T + T)
                    ins = dve.tensor_tensor_scan(s16[:, cols], dt16[:, cols], dt16[:, cols], 0.0, ALU.add, ALU.bypass)
                dve_a.done(ins, "sum")
                after(dve, dve_a, q, "sum")
                dve_a.done(dve.tensor_scalar(dt16[:, :], s16[:, :], neg_a[:, :], CUM_EPS_LOG, ALU.mult, ALU.max), "cum")

            def cb(q):
                after(dve, act_a, q, "p")
                dve.tensor_tensor(c16[:, :], c16[:, :], e16[:, :], ALU.mult)
                dve_a.done(dve.tensor_tensor(b16[:, :], b16[:, :], s16[:, :], ALU.mult), "qk")

            def mt_part(q, b):
                after(dve, pe_a, q, f"mt{b}")
                dve.tensor_tensor(mt[:, 0:T], a_bank[:, 0:T], field("causal"), ALU.mult)
                dve_a.done(dve.tensor_tensor(mt[0:TAIL, T:T + TAIL], a_bank[0:TAIL, T:T + TAIL],
                                             field("causal", TAIL)[:, 0:TAIL], ALU.mult), f"mt{b}")

            def y(q, b):
                after(dve, pe_a, q, f"y{b}")
                cols = slice(b * T, b * T + T)
                for k in range(2):
                    ins = dve.scalar_tensor_tensor(th[:, k, cols], xc[:, k, cols], field("skip_d")[:, k:k + 1],
                                                   a_bank[:, k * T:k * T + T], ALU.mult, ALU.add)
                dve_a.done(ins, f"y{b}")
                after(dve, dve_a, q, f"y{b}")
                dve_a.done(dve.tensor_tensor(gate[:, :, cols], th[:, :, cols], gate[:, :, cols], ALU.mult), f"yg{b}")

            def out_proj(q):
                after(dve, pe_a, q, "out")
                dve_a.done(dve.scalar_tensor_tensor(h_a[:, 0:PT], a_bank[:, 0:PT], field("out_b"), h_a[:, 0:PT],
                                                    ALU.add, ALU.add), "out")

            def top8(who, pe_, where, bias, lg_, top_, top_i_, tag):
                def part(q):
                    after(dve, pe_, q, "logits")
                    who.done(dve.tensor_tensor(lg_[:, :, :], where[:, 0:24].rearrange("p (c e) -> p c e", c=3),
                                               spread(field(bias), 1, 3), ALU.add), "lg")
                    after(dve, who, q, "lg")
                    plain(dve)
                    for c in range(3):
                        ins = dve.max(top_[:, c, :], lg_[:, c, :])
                    who.done(ins, "top")
                    after(dve, who, q, "top")
                    plain(dve)
                    for c in range(3):
                        ins = dve.max_index(top_i_[:, c, :], top_[:, c, :], lg_[:, c, :])
                    who.done(ins, "top_i")
                    after(dve, who, q, "top_i")
                return part

            top_a = top8(dve_a, pe_a, a_bank, "router_b", lg, top, top_i, "a")
            top_cc = top8(dve_c, pe_c, c_bank, "gate_b", lg_c, top_c, top_ic, "c")

            def route(q):
                top_a(q)
                dve.tensor_copy(top_f[:, :, :], top_i[:, :, 0:2])
                dve_a.done(dve.tensor_tensor(e_gap[:, :], top[:, :, 1], top[:, :, 0], ALU.subtract), "gap")

            def weights(q):
                after(dve, dve_a, q, "gap")
                hot = ow[:, :, 8:24].rearrange("p c (k e) -> p c k e", k=2)
                for c in range(3):
                    dve.tensor_tensor(hot[:, c, :, :], spread(field("iota"), 1, 2), spread(top_f[:, c, :], 2, E), ALU.is_equal)
                after(dve, act_a, q, "e_gap")
                dve_a.done(dve.tensor_scalar(e_sum[:, :], e_gap[:, :], 1.0, None, ALU.add), "e_sum")
                after(dve, dve_a, q, "e_sum")
                dve_a.done(dve.reciprocal(ow[:, :, 24], e_sum[:, :]), "w0")
                after(dve, dve_a, q, "w0")
                dve_a.done(dve.tensor_tensor(ow[:, :, 25], e_gap[:, :], ow[:, :, 24], ALU.mult), "w1")
                after(dve, dve_a, q, "w1")
                dve.tensor_tensor(ow_w[:, :, :], ow[:, :, 8:16], ow[:, :, 24:25].broadcast_to([128, 3, 8]), ALU.mult)
                dve_a.done(dve.tensor_tensor(ow[:, :, 0:8], ow[:, :, 16:24], ow[:, :, 25:26].broadcast_to([128, 3, 8]),
                                             ALU.mult), "ow1")
                after(dve, dve_a, q, "ow1")
                dve_a.done(dve.tensor_tensor(ow[:, :, 0:8], ow[:, :, 0:8], ow_w[:, :, :], ALU.add), "ow")

            def owt(q):
                after(dve, act_a, q, "owt")
                dve_a.done(dve.tensor_copy(ow_b[:, :], a_bank[0:24, 0:PT]), "owt")

            def bo(q):
                after(dve, pe_a, q, "bo")
                dve_a.done(dve.tensor_tensor(h_a[:, 0:PT], h_a[:, 0:PT], a_bank[:, 0:PT], ALU.add), "bo")

            def take_b(q):
                after(dve, dve_a, q, "bo")
                before(dve, dve_b, q, "h2_1")
                dve.tensor_copy(h1[:, :], h_a[:, 0:PT])
                after(dve, act_a, q, "back2")
                before(dve, pool_b, q, f"mx{PAIR_UNITS - 1}")
                dve_b.done(dve.tensor_copy(xb_hi[:, :], xn_a[:, 0:PT]), "take_hi")
                after(dve, dve_b, q, "take_hi")
                dve_b.done(dve.tensor_tensor(xb_lo[:, :], xn_a[:, 0:PT], xb_hi[:, :], ALU.subtract), "take_lo")

            def cell(q, u):
                e = u % E
                after(dve, act_b, q, f"i{u}")
                dve.scalar_tensor_tensor(act4[:, 0, :], act4[:, 0, :], 1.0, cell2[:, e, :], ALU.add, ALU.mult)
                after(dve, act_b, q, f"g{u}")
                dve_b.done(dve.scalar_tensor_tensor(act4[:, 2, :], act4[:, 1, :], 1.0, act4[:, 2, :], ALU.add, ALU.mult),
                           f"ig{u}")
                after(dve, dve_b, q, f"ig{u}")
                dve_b.done(dve.scalar_tensor_tensor(cell2[:, e, :], act4[:, 0, :], 0.5, act4[:, 2, :], ALU.mult, ALU.add),
                           f"c{u}")

            def hidden(q, u):
                e = u % E
                after(dve, act_b, q, f"tc{u}")
                dve_b.done(dve.scalar_tensor_tensor(hid2[:, :], act4[:, 3, :], 1.0, hid2[:, :], ALU.add, ALU.mult), f"h{u}")
                after(dve, dve_b, q, f"h{u}")
                dve_b.done(dve.tensor_copy(hh[:, e, :], hid2[:, :]), f"hh{u}")
                if u:
                    after(dve, pe_b, q, f"z{u - 1}")
                else:
                    before(dve, pe_b, q, f"z{PAIR_UNITS - 1}")
                hs = u // 4
                if u % 4 == 0:
                    dve.wait_ge(onehot_in[hs % 2], q * 32 + 16 * (hs // 2) + 16)
                dve_b.done(dve.tensor_tensor(two(hm[:, :]), two(hid2[:, :]), onehot[hs % 2][:, e % 4, :, :], ALU.mult),
                           f"hm{u}")

            def step_out(q, b):
                after(dve, pe_b, q, f"z{E * b + E - 1}")
                dve.wait_ge(slot_w_in[b], q * 16 + 16)
                dve_b.done(dve.tensor_tensor(z_tmp[:, :, :], two(z_bank[:, 0:PT]), slot_w[b][:, :, :], ALU.mult), f"zz{b}")
                after(dve, dve_b, q, f"zz{b}")
                cols = slice(b * T, b * T + T)
                dve_b.done(dve.tensor_tensor(z_tmp[:, 0, :], z_tmp[:, 0, :], z_tmp[:, 1, :], ALU.add), f"sum{b}")
                after(dve, dve_b, q, f"sum{b}")
                dve_b.done(dve.tensor_tensor(h2[:, cols], h1[:, cols], z_tmp[:, 0, :], ALU.add), f"h2_{b}")

            def take_c(q):
                after(dve, dve_b, q, "h2_1")
                before(dve, pe_c, q, "emit")
                dve_c.done(dve.tensor_copy(h_c[:, 0:PT], h2[:, :]), "take")

            def qk(q, w, p):
                after(dve, act_c, q, f"{w}{p}")
                dst = (qs if w == "q" else ks)[:, p, 0:PT]
                n = turn(w, p)
                dve_c.done(dve.scalar_tensor_tensor(dst, qk_hi(n), field(f"{w}_lo"), qk_bank(n)[:, 0:PT], ALU.mult, ALU.add),
                           f"{w}{p}")

            def v(q, b):
                after(dve, act_c, q, f"v{b}")
                own = spread(spread(field("own_row"), 1, 2), 3, HD)
                dve_c.done(dve.tensor_tensor(v_tail[:, :, :].rearrange("p g (j d) -> p g j d", j=4)[:, :, :, 0:HD],
                                             c_bank[:, 128:256].rearrange("p (g j d) -> p g j d", g=2, j=4), own, ALU.mult),
                           f"v{b}")

            def smax(q, b, m):
                after(dve, pe_c, q, f"s{m}_{b}")
                for side, where in enumerate((c_bank, m_bank)):
                    hs = heads_of(m, side)
                    ins = dve.tensor_reduce(row_max[:, hs[0]:hs[-1] + 1:2], per_head(where, len(hs)), AX.X, ALU.max)
                if m:
                    ins = dve.tensor_reduce(tail_max[:, :], per_head(c_bank, 3)[:, 1:3], AX.X, ALU.max)
                dve_c.done(ins, f"s{m}_{b}")
                if m:
                    after(dve, dve_c, q, f"s1_{b}")
                    dve_c.done(dve.tensor_tensor(tail_max_own[:, :, :], spread(tail_max[:, :], 2, 4),
                                                 spread(field("own_row"), 1, 2), ALU.mult), f"own_{b}")

            def pv(q, b):
                after(dve, pe_c, q, f"pv{b}")
                plain(dve)
                src = m_bank[:, 0:2 * (T + 1)].rearrange("p (g t) -> p g t", t=T + 1)[:, :, 0:T]
                cols = slice(b * T, b * T + T)
                dve_c.done(dve.stream_shuffle(norm[:, :, cols], src, [HD + i % HD for i in range(32)]), f"den{b}")
                after(dve, dve_c, q, f"den{b}")
                dve_c.done(dve.reciprocal(norm[:, :, cols], norm[:, :, cols]), f"inv{b}")
                after(dve, dve_c, q, f"inv{b}")
                dve_c.done(dve.tensor_tensor(o_n[:, :, cols], src, norm[:, :, cols], ALU.mult), f"on{b}")

            def proj(q):
                after(dve, pe_c, q, "proj")
                dve_c.done(dve.tensor_tensor(h_c[:, 0:PT], h_c[:, 0:PT], c_bank[:, 0:PT], ALU.add), "proj")

            def moe_gate(q):
                top_cc(q)
                dve_c.done(dve.tensor_copy(top_fc[:, :, :], top_ic[:, :, 0:1]), "top_f")
                after(dve, dve_c, q, "top_f")
                dve_c.done(dve.tensor_tensor(oh_c[:, :, :], spread(field("iota"), 1, 3),
                                             top_fc[:, :, 0:1].broadcast_to([128, 3, E]), ALU.is_equal), "oh")

            def oht(q):
                after(dve, act_c, q, "oht")
                dve_c.done(dve.tensor_scalar(oh_b[:, :], c_bank[0:8, 0:PT], -1.0, None, ALU.add), "oht")

            def emit(q):
                after(dve, pe_c, q, f"down{2 * E - 1}")
                dve_c.done(dve.tensor_tensor(h_c[:, 0:PT], h_c[:, 0:PT], m_bank[:, 0:PT], ALU.add), "moe")

            ln_args_a = (dve_a, pe_a, pool_a, a_bank, stats, mv, rstd, xt_a)
            ln_args_c = (dve_c, pe_c, pool_c, c_bank, stats_c, mv_c, rstd_c, xt_c)
            run(dve, {("A", "tok"): tok, ("A", "ln"): ln(*ln_args_a),
                      ("A", "ln_x"): ln_x(dve_a, pool_a, a_bank, mv, rstd, xt_a),
                      ("A", "in"): silu_res, ("A", "conv"): conv, ("A", "xc"): silu_x, ("A", "scan"): scan, ("A", "cb"): cb,
                      ("A", "mt"): mt_part, ("A", "weights"): weights,
                      ("A", "y"): y, ("A", "out"): out_proj, ("A", "route"): route, ("A", "owt"): owt, ("A", "bo"): bo,
                      ("B", "take"): take_b, ("B", "cell"): cell, ("B", "hidden"): hidden, ("B", "step_out"): step_out,
                      ("C", "take"): take_c, ("C", "ln"): ln(*ln_args_c),
                      ("C", "ln_x"): ln_x(dve_c, pool_c, c_bank, mv_c, rstd_c, xt_c), ("C", "qk"): qk, ("C", "v"): v,
                      ("C", "smax"): smax, ("C", "pv"): pv, ("C", "proj"): proj, ("C", "gate"): moe_gate,
                      ("C", "oht"): oht, ("C", "emit"): emit},
                setup=[lambda c=c: split(c) for c in range(8)] + [first_cells])


def _layout(inputs):
    f = {k: np.asarray(v) for k, v in inputs.items()}
    x = f["x"]
    nb = x.shape[0]
    npairs = nb // 2
    patches = x.reshape(nb, 3, 11, 16, 13, 16).transpose(3, 5, 1, 0, 2, 4).reshape(KC, D, npairs, 2, T - 2)
    x_t = np.zeros((npairs + 1, D, KC, 2, T), np.float32)
    x_t[:npairs, :, :, :, 2:] = patches.transpose(2, 1, 0, 3, 4)
    x_t = x_t.reshape(npairs + 1, D, KC, PT)

    order = [1, 0, 2, 3]
    def gates_first(w):
        return w.reshape(E, D, 4, D)[:, :, order].transpose(1, 0, 2, 3).reshape(D, E * 4 * D)

    p = {name: np.zeros((128, n), np.float32) for name, n in {**FIELDS, **ONCE}.items()}
    p["tok_w"][:] = f["L0_tok_W"].reshape(D, KC, 128).transpose(2, 1, 0).reshape(128, KC * D)
    p["in_w"][:] = f["L0_attn_W_in"]
    x_w = f["L0_attn_W_x"].reshape(2, 128, 2 * DS + 1).transpose(1, 0, 2)
    wx = p["x_w"].reshape(128, 2, 80)
    wx[:, :, 0:DS], wx[:, :, 32:32 + DS], wx[:, :, 64:64 + DS] = x_w[:, :, :DS], x_w[:, :, DS:2 * DS], x_w[:, :, 2 * DS:]
    p["x_b"][0:DS, 0], p["x_b"][32:32 + DS, 0] = f["L0_attn_b_x"][:DS], f["L0_attn_b_x"][DS:2 * DS]
    p["x_b"][64:64 + DS, 0] = f["L0_attn_b_x"][2 * DS]
    p["a_log"][0:DS, 0] = f["L0_attn_A_log"]
    p["out_w"][:] = f["L0_attn_W_out"].reshape(2, 128, D).transpose(1, 0, 2).reshape(128, 2 * D)
    p["out_b"][:, 0] = f["L0_attn_b_out"]
    p["in_b"][:] = f["L0_attn_b_in"].reshape(4, 128).T
    p["conv_w"][:] = f["L0_attn_conv_w"].reshape(2, 128, 4).transpose(1, 0, 2).reshape(128, 8)
    p["conv_b"][:] = f["L0_attn_conv_b"].reshape(2, 128).T
    p["skip_d"][:] = f["L0_attn_D"].reshape(2, 128).T
    p["tok_b"][:, 0] = f["L0_tok_b"]
    p["cls_a"][:, 0], p["cls_b"][:, 0] = f["cls_tok"].reshape(D), f["L0_tok_cls_token"].reshape(D)
    p["pos"][:] = f["L0_tok_pos_emb"].reshape(1, T - 1)
    p["lstm_out_w"][:] = f["L0_ffn_Wo"].transpose(1, 0, 2).reshape(128, E * D)
    p["lstm_b"][:] = f["L0_ffn_b"].reshape(E, 4, D)[:, order].transpose(2, 0, 1).reshape(128, 4 * E)
    p["router_w"][:], p["router_b"][:] = f["L0_ffn_router_w"], f["L0_ffn_router_b"]
    p["gate_w"][:], p["gate_b"][:] = f["L1_ffn_Wg"], f["L1_ffn_bg"]
    p["bo"][0:E], p["b2"][0:E] = f["L0_ffn_bo"], f["L1_ffn_b2"]
    p["w1_b"][:] = f["L1_ffn_b1"].reshape(2 * E, 128).T
    qkv = f["L1_attn_w_qkv"].reshape(D, NH, 3, HD)
    for name, part in (("q_w", 0), ("k_w", 1)):
        p[name].reshape(D, NH, 4, HD)[:, :, 0:3] = qkv[:, :, part][:, :, None]
    p["v_w"][:] = qkv[:, :, 2].reshape(D, D)
    p["q_lo"].reshape(2, 4, 16)[:, 2] = -1.0
    p["k_lo"].reshape(2, 4, 16)[:, 1] = -1.0
    p["proj_w"].reshape(4, 32, 2, D)[:, 0:HD] = f["L1_attn_w_proj"].reshape(2, 4, HD, D).transpose(1, 2, 0, 3)

    row, col = np.arange(128)[:, None], np.arange(T)[None]
    p["ident"][:] = np.eye(128)
    p["causal"][:] = col >= row
    p["band_main"][:] = np.where(128 + col[:, :18] - row > 128, -1e9, 0.0)
    p["band_tail"][:] = np.where((128 + row % 32) - col[:, :18] > 128, -1e9, 0.0)
    pair_, j = np.arange(4)[:, None], np.arange(4)[None]
    p["own_cols"][:] = (j == 2 * (pair_ % 2) + row[:, :, None] // 64).reshape(128, 16)
    p["own_row"][:] = (j == row // 32) & (row % 32 < TAIL)
    p["tail_sel"][:] = (row % 32 == col[:, :18]) & (col[:, :18] < TAIL)
    p["iota"][:] = np.arange(E)
    p["minus_half"][:] = -0.5
    heads = p["tail_heads"].reshape(128, 2, 4, 32)
    for h in range(NH):
        heads[h, h // 4, h % 4, 0:TAIL] = 1.0
    packed, once = (np.concatenate([p[name] for name in names], axis=1) for names in (FIELDS, ONCE))

    v_ones = np.zeros((128, 512), np.float32)
    v_ones[:, :256].reshape(128, NH, 2, HD)[:, :, 1] = 1.0
    v_ones[:, 256:].reshape(128, 2, 4, 2, HD)[:, :, :, 1] = p["own_row"][:, None, :, None]
    w1 = f["L1_ffn_W1"]
    w2 = f["L1_ffn_W2"].reshape(E, 2, 128, D).transpose(0, 2, 1, 3).reshape(E, 128, 2 * D)
    return {"x_t": x_t, "wh": gates_first(f["L0_ffn_Wh"]), "wi": gates_first(f["L0_ffn_Wi"]),
            "wmoe": np.concatenate([w1, w2], axis=2), "packed": packed, "once": once, "v_ones": v_ones}


def _program(nc, arrays, nb):
    args = {}
    for name, a in arrays.items():
        args[name] = nc.dram_tensor(f"in_{name}", a.shape, mybir.dt.from_np(a.dtype), kind="ExternalInput").ap()
    args["out"] = nc.dram_tensor("out_0", (nb * T, D), F32, kind="ExternalOutput").ap()
    args["scr_onehot"] = nc.dram_tensor("scr_onehot", (2, E, 2, T), BF16).ap()
    args["scr_weight"] = nc.dram_tensor("scr_weight", (2, 2, T), F32).ap()
    build(nc, **args)


def kernel(**inputs):
    import concourse.bacc as bacc
    from concourse.bass_utils import run_bass_kernel_spmd
    arrays = {k: np.ascontiguousarray(a) for k, a in _layout(inputs).items()}
    nb = np.asarray(inputs["x"]).shape[0]
    nc = bacc.Bacc("TRN2", target_bir_lowering=False, num_devices=1)
    _program(nc, arrays, nb)
    r = run_bass_kernel_spmd(nc, [{f"in_{k}": a for k, a in arrays.items()}], core_ids=[0])
    return r.results[0]["out_0"].reshape(nb, T, D)
```
